# Optimizing a Trainium2 kernel written in Bass

```python
import numpy as np
import jax
import jax.numpy as jnp

def _softmax(x, axis=-1):
    return jax.nn.softmax(x, axis=axis)

def _gelu(x):
    return jax.nn.gelu(x, approximate=True)

def _silu(x):
    return jax.nn.silu(x)

def _sigmoid(x):
    return jax.nn.sigmoid(x)

def _layernorm(x, axis=-1, eps=1e-05):
    m = jnp.mean(x, axis=axis, keepdims=True)
    v = jnp.var(x, axis=axis, keepdims=True)
    return (x - m) / jnp.sqrt(v + eps)

def _scatter_add(tgt, idx, src, axis=0):
    return tgt.at[idx].add(src)

def _segment_sum(src, seg, n):
    return jax.ops.segment_sum(src, seg, n)
kernel_name = 'mk_adj_ffn_d1_adj_r2_a0482b'

def setup_inputs(seed: int=0):
    np.random.seed(seed)
    _w = jnp.asarray

    def _rec_inputs():
        import jax
        import jax.numpy as jnp
        _gk = jax.random.key(seed)
        x = -0.0002928 + 1 * jax.random.normal(jax.random.fold_in(_gk, 1), (3327, 256), jnp.float32)
        _a = jax.random.bernoulli(jax.random.fold_in(_gk, 2), 0.00961827, (3327, 3327))
        _a = jnp.logical_or(_a, jnp.eye(3327, dtype=bool))
        _af = _a.astype(jnp.float32)
        _af = _af * jax.random.uniform(jax.random.fold_in(_gk, 3), (3327, 3327), jnp.float32, 0.05, 1)
        adj = _af
        return (x, adj)
    x, adj = _rec_inputs()

    def _L0_gnn_setup():
        import jax, jax.numpy as jnp
        import numpy as np
        N = 4096
        D = 256
        key = jax.random.key(seed)
        k1, k2 = jax.random.split(key)
        inp = jax.random.normal(k1, (N, D), dtype=jnp.float32)
        A = jax.random.uniform(k2, (N, N), dtype=jnp.float32)
        W = jnp.ones((D,), dtype=jnp.float32)
        return {'input': inp, 'A': A, 'W': W}
    _L0_gnn_all = _L0_gnn_setup()
    _L0_gnn_in = {k: v for k, v in _L0_gnn_all.items() if k in ('W',)}
    del _L0_gnn_all

    def _L0_ffn_setup():
        import jax, jax.numpy as jnp
        import numpy as np
        D_MODEL = 256
        HIDDEN = 1024
        N_EXPERTS = 8
        TOP_K = 2
        key = jax.random.key(seed)
        ks = jax.random.split(key, 7)
        B, S = (4, 1024)
        s1 = 1.0 / np.sqrt(D_MODEL)
        s2 = 1.0 / np.sqrt(HIDDEN)
        return {'x': jax.random.normal(ks[0], (B, S, D_MODEL), dtype=jnp.float32), 'W1': jax.random.normal(ks[1], (N_EXPERTS, D_MODEL, HIDDEN), dtype=jnp.float32) * s1, 'b1': jnp.zeros((N_EXPERTS, HIDDEN), dtype=jnp.float32), 'W2': jax.random.normal(ks[2], (N_EXPERTS, HIDDEN, D_MODEL), dtype=jnp.float32) * s2, 'b2': jnp.zeros((N_EXPERTS, D_MODEL), dtype=jnp.float32), 'Wg': jax.random.normal(ks[3], (D_MODEL, N_EXPERTS), dtype=jnp.float32) * s1, 'bg': jnp.zeros((N_EXPERTS,), dtype=jnp.float32)}
    _L0_ffn_all = _L0_ffn_setup()
    _L0_ffn_in = {k: v for k, v in _L0_ffn_all.items() if k in ('W1', 'b1', 'W2', 'b2', 'Wg', 'bg')}
    del _L0_ffn_all
    return {'x': x, 'adj': adj, 'L0_gnn_W': _L0_gnn_in['W'], 'L0_ffn_W1': _L0_ffn_in['W1'], 'L0_ffn_b1': _L0_ffn_in['b1'], 'L0_ffn_W2': _L0_ffn_in['W2'], 'L0_ffn_b2': _L0_ffn_in['b2'], 'L0_ffn_Wg': _L0_ffn_in['Wg'], 'L0_ffn_bg': _L0_ffn_in['bg']}

def reference(x, adj, L0_gnn_W, L0_ffn_W1, L0_ffn_b1, L0_ffn_W2, L0_ffn_b2, L0_ffn_Wg, L0_ffn_bg):
    import jax
    import jax.numpy as jnp

    def _L0_gnn_ref(input, A, W):
        import jax, jax.numpy as jnp
        import numpy as np
        N = 4096
        D = 256
        hidden = input * W
        return A @ hidden

    def _L0_ffn_ref(x, W1, b1, W2, b2, Wg, bg):
        import jax, jax.numpy as jnp
        import numpy as np
        D_MODEL = 256
        HIDDEN = 1024
        N_EXPERTS = 8
        TOP_K = 2
        gate_scores = jnp.einsum('bsd,de->bse', x, Wg) + bg
        topk_scores, topk_idx = jax.lax.top_k(gate_scores, TOP_K)
        topk_weights = jax.nn.softmax(topk_scores, axis=-1)
        h = jax.nn.relu(jnp.einsum('bsd,edh->bseh', x, W1) + b1)
        expert_outputs = jnp.einsum('bseh,ehd->bsed', h, W2) + b2
        topk_out = jnp.take_along_axis(expert_outputs, topk_idx[..., None], axis=-2)
        return jnp.sum(topk_out * topk_weights[..., None], axis=-2)
    x = x + _L0_gnn_ref(_layernorm(x, axis=-1), adj, L0_gnn_W)
    x = x + _L0_ffn_ref(_layernorm(x, axis=-1)[None], L0_ffn_W1, L0_ffn_b1, L0_ffn_W2, L0_ffn_b2, L0_ffn_Wg, L0_ffn_bg)[0]
    return x

_drawn_inputs = setup_inputs


def setup_inputs(seed=0):
    import zlib

    import numpy as np

    out = dict(_drawn_inputs(seed))
    spreads = {'L0_gnn_W': (1.0, 0.2),
     'L0_ffn_b1': (0.0, 0.579),
     'L0_ffn_b2': (0.0, 0.409),
     'L0_ffn_bg': (0.0, 0.1)}
    factors = {}
    for name, (base, spread) in spreads.items():
        noise = np.random.default_rng([zlib.crc32(name.encode()), seed]).standard_normal(out[name].shape)
        drawn = base * np.exp(spread * noise) if base else spread * noise
        out[name] = jnp.asarray(drawn.astype(out[name].dtype))
    for name, factor in factors.items():
        out[name] = (out[name] * factor).astype(out[name].dtype)
    return out
```

```python
import concourse.bass as bass
from concourse import mybir
from contextlib import ExitStack


f32 = mybir.dt.float32
f16 = mybir.dt.float16
bf16 = mybir.dt.bfloat16
i32 = mybir.dt.int32
u32 = mybir.dt.uint32
ALU = mybir.AluOpType
ACT = mybir.ActivationFunctionType
AX = mybir.AxisListType

P = 128
N = 3327
D = 256
H = 1024
E = 8
TOPK = 2
EPS = 1e-5
NT = (N + P - 1) // P
NP = NT * P
LAST = N - (NT - 1) * P
LAST16 = LAST // 16 * 16
KD = D // P
KH = H // P

GROUPS = [(0, 5), (5, 5), (10, 4), (14, 4), (18, 4), (22, 4)]
NG = len(GROUPS)
GW = 5 * P
NBUF = 3
AHEAD = 2
PAIRS = NT // 2

S_ADJ = 2.0 ** 6
S_HID = 2.0 ** 4
S_W = 2.0 ** 8
S_X = 2.0 ** 5
S_H = 2.0 ** 4

TILES = (TOPK * N + E * (P - 1)) // P
LEAST = (TOPK * N + P - 1) // P
CAP = (N + P - 1) // P * P + P
SPARE = E * CAP
DUMP = SPARE + (TILES - LEAST) * P
XROWS = DUMP + TOPK
C_SLO, C_SHI, C_ELO, C_TOK, XW = D, D + 1, D + 2, D + 3, D + 4
ZROWS = 3 * NP + P


def gnn_moe(nc, x, adj, gnn_w, w1, b1, w2, b2, wg, bg, out):
    ctx = ExitStack()
    with ctx:
        def sb(name, shape, dt):
            return ctx.enter_context(nc.sbuf_tensor(name, shape, dt))

        def pb(name, shape, dt=f32):
            return ctx.enter_context(nc.psum_tensor(name, shape, dt))

        def sem(name):
            return ctx.enter_context(nc.semaphore(name))

        x_rows = nc.dram_tensor("x_rows", [XROWS, XW], f32, kind="Internal").ap()
        x1_rows = nc.dram_tensor("x1_rows", [NP, D], f32, kind="Internal").ap()
        z_rows = nc.dram_tensor("z_rows", [ZROWS, D], f32, kind="Internal").ap()

        w1s = sb("w1s", [P, E, 2, KD, H], f16)
        w2s = sb("w2s", [P, E, KH, 2, D], f16)
        hid = sb("hid", [P, NT, 2, D], f16)
        adj_in = sb("adj_in", [P, 2, NP], f32)
        adjT = sb("adjT", [P, NBUF, 2, GW], f16)
        wst = sb("wst", [P, 2, H], f32)
        xin = sb("xin", [P, 2, D], f32)
        row = sb("row", [P, 2, XW], f32)
        padrow = sb("padrow", [P, XW], f32)
        x1T = sb("x1T", [P, KD, P], f32)
        ident = sb("ident", [P, P], f32)
        before = sb("before", [P, P], bf16)
        ones = sb("ones", [P, P], bf16)
        wrow = sb("wrow", [P, D], f32)
        wgs = sb("wgs", [P, KD, E], f32)
        bgs = sb("bgs", [P, E], f32)
        b1r = sb("b1r", [E * KH, P], f32)
        b1t = sb("b1t", [P, E * KH], f32)
        stats = sb("stats", [P, 2, 6], f32)
        mv = sb("mv", [P, 2, 2], f32)
        sd = sb("sd", [P, 2], f32)
        rstd = sb("rstd", [P, 2], f32)
        shift = sb("shift", [P, 2], f32)
        iota_i = sb("iota_i", [P, TILES], i32)
        iota_e = sb("iota_e", [P, E], f32)
        iota_t = sb("iota_t", [P, TILES], f32)
        region = sb("region", [P, E], f32)
        tok_i = sb("tok_i", [P, NT], i32)
        tok = sb("tok", [P, NT], f32)
        live = sb("live", [P, NT], f32)
        dump = sb("dump", [P, NT, TOPK], f32)
        pad_i = sb("pad_i", [P, 1], i32)
        score = sb("score", [P, E], f32)
        top = sb("top", [P, E], f32)
        below = sb("below", [P, E], f32)
        topix = sb("topix", [P, E], u32)
        topf = sb("topf", [P, TOPK], f32)
        ehi = sb("ehi", [P, 1], f32)
        hot = sb("hot", [P, TOPK, E], f32)
        both = sb("both", [P, E], bf16)
        count = sb("count", [P, 2, E], bf16)
        place = sb("place", [P, E], f32)
        junk = sb("junk", [P, TOPK, E], f32)
        posf = sb("posf", [P, TOPK], f32)
        pos = sb("pos", [P, 2, TOPK], i32)
        epsc = sb("epsc", [P, 1], f32)
        x_all = w2s[:, E // 2:E].rearrange("p e k s d -> p (e k s d)").bitcast(f32)[:, 0:NT * D] \
            .rearrange("p (t d) -> p t d", t=NT)
        hid32 = wst[:, :, :].rearrange("p a (b d) -> p a b d", b=4)

        tp = [pb(f"tp{i}", [P, 1024]) for i in range(2)]
        acc = [pb(f"acc{i}", [P, 2, D]) for i in range(2)]
        small = pb("small", [P, 512])
        gate_ps = pb("gate_ps", [P, 512])
        scores_ps = gate_ps[:, 0:E]
        rank_ps = gate_ps[:, 128:128 + E]
        total_ps = gate_ps[:, 256:256 + E]

        const_set, const_ld = sem("const_set"), sem("const_ld")
        x_in, tail_zero = sem("x_in"), sem("tail_zero")
        stats1, mv1, sd1, rstd1, shift1, norm1, hid32_rdy, hid_hi, hid_lo = [
            sem(s) for s in ("stats1", "mv1", "sd1", "rstd1", "shift1", "norm1", "hid32_rdy", "hid_hi", "hid_lo")]
        adj_ld = [sem(f"adj_ld{i}") for i in range(2)]
        tposed, adj_hi, adj_lo, mm_done = [sem(s) for s in ("tposed", "adj_hi", "adj_lo", "mm_done")]
        xin_ld = [sem(f"xin_ld{i}") for i in range(2)]
        x1_st = [sem(f"x1_st{i}") for i in range(2)]
        x1a, x1b, st2, mv2, sd2, rstd2, norm2, tok_rdy = [
            sem(s) for s in ("x1a", "x1b", "st2", "mv2", "sd2", "rstd2", "norm2", "tok_rdy")]
        nT_done, nT_rdy, gate_done = sem("nT_done"), sem("nT_rdy"), sem("gate_done")
        sc_rdy, top_rdy, below_rdy, ix_rdy, ixf_rdy, e_rdy, hot_rdy, both_rdy, slo_rdy, count_rdy = [
            sem(s) for s in ("sc_rdy", "top_rdy", "below_rdy", "ix_rdy", "ixf_rdy", "e_rdy", "hot_rdy", "both_rdy", "slo_rdy",
                             "count_rdy")]
        rank_done, place_rdy, posf_rdy, pos_rdy = [
            sem(s) for s in ("rank_done", "place_rdy", "posf_rdy", "pos_rdy")]
        sent = [sem(f"sent{i}") for i in range(2)]
        spare_st = sem("spare_st")
        w_ld = [sem(f"w_ld{i}") for i in range(2)]
        w_sc, w_hi, w_lo = sem("w_sc"), sem("w_hi"), sem("w_lo")

        def need(eng, s, v):
            if not isinstance(v, int) or v > 0:
                eng.wait_ge(s, v)

        def hold(eng):
            eng.nop(nofuse=True)

        def pairs(eng, body):
            body(0, False)
            body(1, True)
            with eng.Fori(2, E + 1) as r:
                body(r, True)
            with eng.Fori(E + 1, PAIRS - 1) as r:
                body(r, False)
            body(PAIRS - 1, False)

        def load_rows(eng, dst, src, i, s):
            if isinstance(i, int) and i == NT - 1:
                eng.dma_start(dst[0:LAST16], src[i * P:i * P + LAST16, :]).then_inc(s, 16)
                eng.dma_start(dst[LAST16:LAST], src[i * P + LAST16:N, :]).then_inc(s, 16)
            else:
                eng.dma_start(dst, src[bass.ds(i * P, P), :]).then_inc(s, 16)

        def two(i):
            return 2 if isinstance(i, int) and i == NT - 1 else 1

        with nc.Block() as block:

            @block.sync
            def _(sp):
                sp.wait_ge(tail_zero, 1)
                sp.dma_start(x_all[:, 0:NT - 1, :],
                             x[0:(NT - 1) * P, :].rearrange("(t p) d -> p t d", p=P)).then_inc(x_in, 16)
                load_rows(sp, x_all[:, NT - 1, :], x, NT - 1, x_in)
                sp.dma_start(wrow[:, :], gnn_w.rearrange("(a d) -> a d", a=1).to_broadcast((P, D))) \
                    .then_inc(const_ld, 16)
                sp.dma_start(wgs[:, :, :], wg.rearrange("(k p) e -> p k e", p=P)).then_inc(const_ld, 16)
                sp.dma_start(bgs[:, :], bg.rearrange("(a e) -> a e", a=1).to_broadcast((P, E))) \
                    .then_inc(const_ld, 16)
                sp.dma_start(b1r[:, :], b1.rearrange("e (c p) -> (e c) p", p=P)).then_inc(const_ld, 16)

                def load_weights(e, u):
                    src = w1[bass.ds(e, 1), u * P:(u + 1) * P, :].rearrange("a p h -> p (a h)") if u < KD else \
                        w2[bass.ds(e, 1), (u - KD) * 4 * P:(u - KD + 1) * 4 * P, :] \
                        .rearrange("a (c p) d -> p (a c) d", p=P)
                    dst = wst[:, u % 2, :] if u < KD else wst[:, u % 2, :].rearrange("p (c d) -> p c d", c=4)
                    sp.dma_start(dst, src).then_inc(w_ld[u % 2], 16)

                def body(r, weights):
                    for s in range(2):
                        i = 2 * r + s
                        need(sp, tposed, NG * (i - 1))
                        load_rows(sp, adj_in[:, s, 0:N], adj, i, adj_ld[s])
                        if not (isinstance(i, int) and i < 2):
                            store_x1(i - 2, s)
                            sp.wait_ge(x1_st[s], 16 * r)
                            sp.wait_ge(norm2, i - 1)
                        load_rows(sp, xin[:, s, :], x, i, xin_ld[s])
                        if weights:
                            for u in (2 * s, 2 * s + 1):
                                sp.wait_ge(w_lo, 4 * r + u - 2 - 1)
                                load_weights(r - 1, u)

                def store_x1(i, s):
                    sp.wait_ge(x1b, i + 1)
                    sp.dma_start(x1_rows[bass.ds(i * P, P), :], xin[:, s, :]).then_inc(x1_st[s], 16)

                pairs(sp, body)
                for s in range(2):
                    store_x1(NT - 2 + s, s)
                for s in range(2):
                    sp.wait_ge(x1_st[s], 16 * PAIRS)

            @block.scalar
            def _(act):
                for j in range(PAIRS):
                    k = j % 2
                    act.wait_ge(mv1, 2 * (j + 1))
                    act.wait_ge(const_set, 1)
                    nc.scalar.activation(sd[:, :], mv[:, :, 1], ACT.Sqrt, bias=epsc[:, :]).then_inc(sd1, 1)
                    act.wait_ge(shift1, j + 1)
                    for b in range(2):
                        need(act, hid_lo, j - 1)
                        nc.scalar.activation(hid32[:, k, b, :], x_all[:, 2 * j + b, :], ACT.Identity,
                                             bias=shift[:, b:b + 1], scale=rstd[:, b:b + 1]).then_inc(norm1, 1)
                    act.wait_ge(hid32_rdy, j + 1)
                    nc.scalar.activation(hid[:, 2 * j:2 * j + 2, 0, :], hid32[:, k, 2:4, :], ACT.Copy,
                                         scale=S_HID).then_inc(hid_hi, 1)

                def body(r, weights):
                    for s in range(2):
                        i = 2 * r + s
                        for g, (b0, nb) in enumerate(GROUPS):
                            n = NG * i + g
                            act.wait_ge(tposed, n + 1)
                            need(act, mm_done, n - NBUF + 1)
                            nc.scalar.activation(adjT[:, g % NBUF, 0, 0:nb * P], tp[g % 2][:, 0:nb * P],
                                                 ACT.Copy, scale=S_ADJ).then_inc(adj_hi, 1)
                            if g == 2 and not (isinstance(i, int) and i == 0):
                                root(i - 1, 1 - s)
                            if g == 4 and not (isinstance(i, int) and i == 0):
                                gate_in(i - 1)
                            if weights and g in (1, 4):
                                split(r - 1, 2 * s + (g == 4))

                def root(i, s):
                    act.wait_ge(mv2, i + 1)
                    nc.scalar.activation(sd[:, 0:1], mv[:, 0, 1:2], ACT.Sqrt, bias=epsc[:, :]).then_inc(sd2, 1)

                def gate_in(i):
                    act.wait_ge(nT_done, i + 1)
                    need(act, gate_done, i)
                    nc.scalar.activation(x1T[:, :, :], small[:, 0:D].rearrange("p (k n) -> p k n", k=KD),
                                         ACT.Copy).then_inc(nT_rdy, 1)

                def split(e, u):
                    unit = 4 * e + u
                    act.wait_ge(w_ld[u % 2], 32 * e + 16 * (u // 2) + 16)
                    nc.scalar.activation(wst[:, u % 2, :], wst[:, u % 2, :], ACT.Copy, scale=S_W).then_inc(w_sc, 1)
                    act.wait_ge(w_sc, unit + 1)
                    dst = w1s[:, bass.ds(e, 1), 0, u, :].rearrange("p a h -> p (a h)") if u < KD else \
                        w2s[:, bass.ds(e, 1), (u - KD) * 4:(u - KD) * 4 + 4, 0, :].rearrange("p a c d -> p (a c) d")
                    src = wst[:, u % 2, :] if u < KD else wst[:, u % 2, :].rearrange("p (c d) -> p c d", c=4)
                    nc.scalar.activation(dst, src, ACT.Copy).then_inc(w_hi, 1)

                pairs(act, body)
                root(NT - 1, 1)
                gate_in(NT - 1)

            @block.gpsimd
            def _(pool):
                nc.gpsimd.memset(x_all[96:P, NT - 1, :], 0.0).then_inc(tail_zero, 1)
                pool.wait_ge(tail_zero, 1)
                nc.gpsimd.memset(epsc[:, :], EPS).then_inc(const_set, 1)
                nc.gpsimd.memset(adj_in[:, :, N:NP], 0.0)
                nc.gpsimd.memset(ident[:, :], 0.0)
                nc.gpsimd.memset(before[:, :], 0.0)
                nc.gpsimd.memset(ones[:, :], 1.0)
                nc.gpsimd.memset(live[:, :], 1.0)
                nc.gpsimd.memset(dump[:, :, :], 0.0)
                nc.gpsimd.memset(padrow[:, :], 0.0)
                nc.gpsimd.memset(count[:, 0, :], 0.0)
                nc.gpsimd.iota(iota_i[:, :], [[1, TILES]], base=0, channel_multiplier=0)
                nc.gpsimd.iota(tok_i[:, :], [[P, NT]], base=0, channel_multiplier=1)
                nc.gpsimd.iota(pad_i[:, :], [[0, 1]], base=2 * NP, channel_multiplier=1).then_inc(const_set, 1)
                pool.wait_ge(const_set, 2)
                nc.gpsimd.affine_select(out=ident[:, :], in_=ident[:, :], compare_op=ALU.not_equal, fill=1.0,
                                        base=0, pattern=[[-1, P]], channel_multiplier=1)
                nc.gpsimd.affine_select(out=before[:, :], in_=before[:, :], compare_op=ALU.is_ge, fill=1.0,
                                        base=0, pattern=[[-1, P]], channel_multiplier=1)
                end = (NT - 1) * P + LAST
                nc.gpsimd.affine_select(out=live[:, :], in_=live[:, :], compare_op=ALU.not_equal, fill=0.0,
                                        base=-end, pattern=[[P, NT]], channel_multiplier=1)
                for c in range(TOPK):
                    nc.gpsimd.affine_select(out=dump[:, :, c], in_=dump[:, :, c], compare_op=ALU.not_equal,
                                            fill=float(DUMP + c), base=-end, pattern=[[P, NT]],
                                            channel_multiplier=1)
                nc.gpsimd.tensor_copy(iota_e[:, :], iota_i[:, 0:E])
                nc.gpsimd.tensor_copy(iota_t[:, :], iota_i[:, :])
                nc.gpsimd.tensor_copy(tok[:, :], tok_i[:, :])
                nc.gpsimd.tensor_scalar(region[:, :], iota_i[:, 0:E], float(CAP), None, ALU.mult)
                nc.gpsimd.tensor_copy(padrow[:, C_TOK:XW], pad_i[:, :]).then_inc(const_set, 1)
                for j in range(PAIRS):
                    k = j % 2
                    pool.wait_ge(const_ld, 64)
                    pool.wait_ge(norm1, 2 * (j + 1))
                    need(pool, hid_lo, j - 1)
                    nc.gpsimd.tensor_tensor(hid32[:, k, 2:4, :], hid32[:, k, 0:2, :],
                                            wrow[:, :].rearrange("p (a d) -> p a d", a=1).to_broadcast((P, 2, D)),
                                            ALU.mult).then_inc(hid32_rdy, 1)
                pool.wait_ge(const_set, 3)
                for c in range(TILES - LEAST):
                    pool.dma_start(x_rows[SPARE + c * P:SPARE + (c + 1) * P, :], padrow[:, :]).then_inc(spare_st, 16)
                pool.wait_ge(hid_lo, PAIRS)
                pool.sem_inc(w_lo, 2)

                def body(r, weights):
                    for s in range(2):
                        i = 2 * r + s
                        for u in ((2 * s, 2 * s + 1) if weights else ()):
                            e = r - 1
                            pool.wait_ge(w_hi, 4 * e + u + 1)
                            src = wst[:, u % 2, :] if u < KD else \
                                wst[:, u % 2, :].rearrange("p (c d) -> p c d", c=4)
                            if u < KD:
                                hi, lo = (w1s[:, bass.ds(e, 1), a, u, :].rearrange("p a h -> p (a h)")
                                          for a in range(2))
                            else:
                                c = (u - KD) * 4
                                hi, lo = (w2s[:, bass.ds(e, 1), c:c + 4, a, :].rearrange("p a c d -> p (a c) d")
                                          for a in range(2))
                            nc.gpsimd.tensor_tensor(lo, src, hi, ALU.subtract).then_inc(w_lo, 1)
                        if not (isinstance(i, int) and i < 2):
                            dispatch(i - 2, s)

                def dispatch(i, s):
                    pool.wait_ge(pos_rdy, i + 1)
                    for c in range(TOPK):
                        hold(pool)
                        nc.gpsimd.indirect_dma_start(
                            out=x_rows, out_offset=bass.IndirectOffsetOnAxis(ap=pos[:, s, c:c + 1].bitcast(u32), axis=0),
                            in_=row[:, s, :], in_offset=None).then_inc(sent[s], 16)

                pairs(pool, body)
                dispatch(NT - 2, 0)
                dispatch(NT - 1, 1)
                pool.wait_ge(spare_st, 16 * (TILES - LEAST))
                for s in range(2):
                    pool.wait_ge(sent[s], 16 * NT)

            def lo_hidden(dve, j):
                dve.wait_ge(hid_hi, j + 1)
                nc.vector.scalar_tensor_tensor(hid[:, 2 * j:2 * j + 2, 1, :], hid32[:, j % 2, 2:4, :], S_HID,
                                               hid[:, 2 * j:2 * j + 2, 0, :], ALU.mult, ALU.subtract) \
                    .then_inc(hid_lo, 1)

            @block.vector
            def _(dve):
                for j in range(PAIRS):
                    k = j % 2
                    if j == 0:
                        dve.wait_ge(x_in, 48)
                    need(dve, norm1, 2 * j)
                    for b in range(2):
                        nc.vector.bn_stats(stats[:, b, :], x_all[:, 2 * j + b, :]).then_inc(stats1, 1)
                    for b in range(2):
                        dve.wait_ge(stats1, 2 * j + b + 1)
                        nc.vector.bn_aggr(mv[:, b, :], stats[:, b, :]).then_inc(mv1, 1)
                    if j:
                        lo_hidden(dve, j - 1)
                    dve.wait_ge(sd1, j + 1)
                    nc.vector.reciprocal(rstd[:, :], sd[:, :]).then_inc(rstd1, 1)
                    dve.wait_ge(rstd1, j + 1)
                    nc.vector.scalar_tensor_tensor(shift[:, :], mv[:, :, 0], -1.0, rstd[:, :], ALU.mult, ALU.mult) \
                        .then_inc(shift1, 1)
                lo_hidden(dve, PAIRS - 1)

                def body(r, weights):
                    for s in range(2):
                        i = 2 * r + s
                        first = isinstance(i, int) and i == 0
                        second = isinstance(i, int) and i < 2
                        for g, (b0, nb) in enumerate(GROUPS):
                            n = NG * i + g
                            dve.wait_ge(adj_hi, n + 1)
                            nc.vector.scalar_tensor_tensor(adjT[:, g % NBUF, 1, 0:nb * P], tp[g % 2][:, 0:nb * P],
                                                           S_ADJ, adjT[:, g % NBUF, 0, 0:nb * P], ALU.mult,
                                                           ALU.subtract).then_inc(adj_lo, 1)
                            if g == 0 and not second:
                                positions(i - 2, s)
                            if g == 1 and not first:
                                residual(i - 1, 1 - s, r if s else r - 1)
                            if g == 2 and not first:
                                normalise(i - 1, 1 - s, r if s else r - 1)
                            if g == 5 and not first:
                                choose(i - 1, 1 - s)

                def residual(i, s, turn):
                    dve.wait_ge(mm_done, NG * (i + 1))
                    dve.wait_ge(xin_ld[s], 16 * turn + 16 * two(i))
                    scale = 1.0 / (S_ADJ * S_HID)
                    nc.vector.scalar_tensor_tensor(xin[:, s, :], acc[s][:, 0, :], scale, xin[:, s, :], ALU.mult,
                                                   ALU.add).then_inc(x1a, 1)
                    dve.wait_ge(x1a, i + 1)
                    nc.vector.scalar_tensor_tensor(xin[:, s, :], acc[s][:, 1, :], scale, xin[:, s, :], ALU.mult,
                                                   ALU.add).then_inc(x1b, 1)
                    dve.wait_ge(x1b, i + 1)
                    nc.vector.bn_stats(stats[:, 0, :], xin[:, s, :]).then_inc(st2, 1)
                    dve.wait_ge(st2, i + 1)
                    hold(dve)
                    nc.vector.bn_aggr(mv[:, 0, :], stats[:, 0, :]).then_inc(mv2, 1)

                def normalise(i, s, turn):
                    dve.wait_ge(sd2, i + 1)
                    nc.vector.reciprocal(rstd[:, 0:1], sd[:, 0:1]).then_inc(rstd2, 1)
                    dve.wait_ge(rstd2, i + 1)
                    need(dve, sent[s], 32 * turn)
                    nc.vector.tensor_scalar(row[:, s, 0:D], xin[:, s, :], mv[:, 0, 0:1], rstd[:, 0:1], ALU.subtract,
                                            ALU.mult).then_inc(norm2, 1)
                    nc.vector.tensor_copy(row[:, s, C_TOK:XW], tok[:, bass.ds(i, 1)]).then_inc(tok_rdy, 1)

                def choose(i, s):
                    dve.wait_ge(gate_done, i + 1)
                    nc.vector.tensor_tensor(score[:, :], scores_ps, bgs[:, :], ALU.add).then_inc(sc_rdy, 1)
                    dve.wait_ge(sc_rdy, i + 1)
                    hold(dve)
                    nc.vector.max(top[:, :], score[:, :]).then_inc(top_rdy, 1)
                    dve.wait_ge(top_rdy, i + 1)
                    nc.vector.tensor_scalar(below[:, :], score[:, :], top[:, 0:1], None, ALU.subtract) \
                        .then_inc(below_rdy, 1)
                    nc.vector.max_index(topix[:, :], top[:, :], score[:, :]).then_inc(ix_rdy, 1)
                    dve.wait_ge(ix_rdy, i + 1)
                    nc.vector.tensor_copy(topf[:, :], topix[:, 0:TOPK]).then_inc(ixf_rdy, 1)
                    dve.wait_ge(ixf_rdy, i + 1)
                    nc.vector.tensor_tensor(row[:, s, C_ELO:C_ELO + 1], topf[:, 0:1], topf[:, 1:2], ALU.min) \
                        .then_inc(e_rdy, 1)
                    nc.vector.tensor_tensor(ehi[:, :], topf[:, 0:1], topf[:, 1:2], ALU.max).then_inc(e_rdy, 1)
                    dve.wait_ge(e_rdy, 2 * i + 2)
                    for c, which in enumerate((row[:, s, C_ELO:C_ELO + 1], ehi[:, :])):
                        nc.vector.tensor_scalar(hot[:, c, :], iota_e[:, :], which, live[:, bass.ds(i, 1)],
                                                ALU.is_equal, ALU.mult).then_inc(hot_rdy, 1)
                    dve.wait_ge(hot_rdy, 2 * i + 2)
                    nc.vector.tensor_tensor(both[:, :], hot[:, 0, :], hot[:, 1, :], ALU.add).then_inc(both_rdy, 1)
                    dve.wait_ge(below_rdy, i + 1)
                    for c in range(TOPK):
                        nc.vector.scalar_tensor_tensor(junk[:, c, :], hot[:, c, :], 1.0, below[:, :], ALU.mult,
                                                       ALU.mult, accum_out=row[:, s, C_SLO + c:C_SLO + c + 1]) \
                            .then_inc(slo_rdy, 1)
                    dve.wait_ge(both_rdy, i + 1)
                    nc.vector.tensor_tensor(count[:, 1 - s, :], count[:, s, :], both[:, :], ALU.add) \
                        .then_inc(count_rdy, 1)

                def positions(i, s):
                    dve.wait_ge(rank_done, i + 1)
                    nc.vector.tensor_tensor(place[:, :], rank_ps, region[:, :], ALU.add).then_inc(place_rdy, 1)
                    dve.wait_ge(place_rdy, i + 1)
                    for c in range(TOPK):
                        nc.vector.scalar_tensor_tensor(junk[:, c, :], hot[:, c, :], 1.0, place[:, :], ALU.mult,
                                                       ALU.mult, accum_out=posf[:, c:c + 1]).then_inc(posf_rdy, 1)
                    dve.wait_ge(posf_rdy, 2 * i + 2)
                    dve.wait_ge(slo_rdy, 2 * i + 2)
                    dve.wait_ge(tok_rdy, i + 1)
                    nc.vector.tensor_tensor(pos[:, s, :], posf[:, :],
                                            dump[:, bass.ds(i, 1), :].rearrange("p a c -> p (a c)"),
                                            ALU.add).then_inc(pos_rdy, 1)

                dve.wait_ge(const_set, 3)
                dve.wait_ge(const_ld, 64)
                pairs(dve, body)
                positions(NT - 2, 0)
                residual(NT - 1, 1, PAIRS - 1)
                normalise(NT - 1, 1, PAIRS - 1)
                choose(NT - 1, 1)
                positions(NT - 1, 1)

            @block.tensor
            def _(pe):
                def turn_adj(i, s, g, r):
                    b0, nb = GROUPS[g]
                    n = NG * i + g
                    if g == 0:
                        pe.wait_ge(adj_ld[s], 16 * r + 16 * two(i))
                    need(pe, adj_lo, n - 1)
                    for b in range(nb):
                        last = nc.tensor.transpose(tp[g % 2][:, b * P:(b + 1) * P],
                                                   adj_in[:, s, (b0 + b) * P:(b0 + b + 1) * P], ident[:, :])
                    last.then_inc(tposed, 1)

                def product(i, s, g):
                    b0, nb = GROUPS[g]
                    pe.wait_ge(adj_lo, NG * i + g + 1)
                    if isinstance(i, int) and i == 0:
                        pe.wait_ge(hid_lo, (b0 + nb + 1) // 2)
                    if g == 0:
                        need(pe, x1b, i - 1)
                    for b in range(nb):
                        blk = b0 + b
                        nc.tensor.matmul(acc[s][:, :, :], adjT[:, g % NBUF, 0, b * P:(b + 1) * P],
                                         hid[:, blk, :, :], start=(blk == 0), stop=False, skip_group_check=True)
                        last = nc.tensor.matmul(acc[s][:, 1, :], adjT[:, g % NBUF, 1, b * P:(b + 1) * P],
                                                hid[:, blk, 0, :], start=False, stop=(blk == NT - 1),
                                                skip_group_check=True)
                    last.then_inc(mm_done, 1)

                def turn_norm(i, s):
                    pe.wait_ge(norm2, i + 1)
                    need(pe, nT_rdy, i)
                    for k in range(KD):
                        last = nc.tensor.transpose(small[:, k * P:(k + 1) * P], row[:, s, k * P:(k + 1) * P],
                                                   ident[:, :])
                    last.then_inc(nT_done, 1)

                def gate(i):
                    pe.wait_ge(nT_rdy, i + 1)
                    need(pe, sc_rdy, i)
                    for k in range(KD):
                        last = nc.tensor.matmul(scores_ps, x1T[:, k, :], wgs[:, k, :], start=(k == 0),
                                                stop=(k == KD - 1))
                    last.then_inc(gate_done, 1)

                def rank(i, s):
                    pe.wait_ge(both_rdy, i + 1)
                    need(pe, count_rdy, i)
                    need(pe, place_rdy, i)
                    nc.tensor.matmul(rank_ps, before[:, :], both[:, :], start=True, stop=False)
                    nc.tensor.matmul(rank_ps, ones[:, :], count[:, s, :], start=False, stop=True) \
                        .then_inc(rank_done, 1)

                def body(r, weights):
                    for s in range(2):
                        i = 2 * r + s
                        first = isinstance(i, int) and i == 0
                        final = isinstance(i, int) and i == NT - 1
                        for g in range(NG):
                            if g + AHEAD < NG:
                                turn_adj(i, s, g + AHEAD, r)
                            elif not final:
                                turn_adj(i + 1, 1 - s, g + AHEAD - NG, r + s)
                            if not first:
                                if g == 2:
                                    turn_norm(i - 1, 1 - s)
                                if g == 3:
                                    gate(i - 1)
                                if g == 5:
                                    rank(i - 1, 1 - s)
                            product(i, s, g)

                pe.wait_ge(const_set, 3)
                pe.wait_ge(const_ld, 64)
                for g in range(AHEAD):
                    turn_adj(0, 0, g, 0)
                body(0, False)
                with pe.Fori(1, PAIRS - 1) as r:
                    body(r, False)
                body(PAIRS - 1, False)
                turn_norm(NT - 1, 1)
                gate(NT - 1)
                rank(NT - 1, 1)



        def words(region, dt):
            return region.rearrange("p a b c -> p (a b c)").bitcast(dt)

        pool_f = words(hid[:, :, :, :], f32)
        b2s = pool_f[:, 0:E * D]
        at = E * D
        h32 = pool_f[:, at:at + 1024].rearrange("p (a n) -> p a n", a=2)
        at += 1024
        hsp = pool_f[:, at:at + 2048].bitcast(f16).rearrange("p (s v c n) -> p s v c n", s=2, v=2, c=KH)
        at += 2048
        ysum = pool_f[:, at:at + 2 * D].rearrange("p (s d) -> p s d", s=2)
        at += 2 * D
        yrow = pool_f[:, at:at + 2 * D].rearrange("p (s d) -> p s d", s=2)
        pool_t = words(adjT[:, :, :, :], f32)
        xr = pool_t[:, 0:2 * XW].rearrange("p (s w) -> p s w", s=2)
        xT = pool_t[:, 2 * XW:2 * XW + 512].bitcast(f16).rearrange("p (s v k n) -> p s v k n", s=2, v=2, k=KD)
        pool_w = wst[:, :, :].rearrange("p a b -> p (a b)")
        cmp_n = pool_w[:, 0:E * NT].rearrange("p (e k) -> p e k", e=E)
        cmp_t = pool_w[:, 512:512 + TILES * E].rearrange("p (t e) -> p t e", e=E)
        cmp_w = pool_w[:, 1024:1024 + TILES * E].rearrange("p (t e) -> p t e", e=E)
        x1_all = adj_in[:, :, :].rearrange("p a b -> p (a b)").rearrange("p (t d) -> p t d", t=NT)

        thr = sb("thr", [P, NT], f32)
        one_e = sb("one_e", [P, E], f32)
        filled = sb("filled", [P, E], f32)
        cum = sb("cum", [P, E], f32)
        e_raw, start_t, base_f = (pool_w[:, 1536 + 64 * i:1536 + 64 * i + TILES] for i in range(3))
        e_f = sb("e_f", [P, TILES], f32)
        e_i = sb("e_i", [P, TILES], i32)
        base_i = sb("base_i", [P, TILES], i32)
        padat = sb("padat", [P, E], i32)
        sexp = sb("sexp", [P, 2, TOPK], f32)
        ssum = sb("ssum", [P, 2, 1], f32)
        srec = sb("srec", [P, 2, 1], f32)
        high = sb("high", [P, 2, 1], f32)
        zi = sb("zi", [P, 2, 1], i32)
        wd = sb("wd", [P, 2, 1], f32)
        wf = sb("wf", [P, 2, 1], f32)
        wn = sb("wn", [P, 2, 1], f32)
        wt = sb("wt", [P, 2, 1], f32)

        total_done, tstep, tables, b1_done, b1_rdy, b2_ld, pad_st, x1_ld = [
            sem(s) for s in ("total_done", "tstep", "tables", "b1_done", "b1_rdy", "b2_ld", "pad_st", "x1_ld")]
        xr_ld = [sem(f"xr_ld{i}") for i in range(2)]
        xT_done, xT_hi, xT_lo, h_done, h32_rdy, h_hi, h_lo, y_done, ya_rdy, yb_rdy, y_rdy, z_st = [
            sem(s) for s in ("xT_done", "xT_hi", "xT_lo", "h_done", "h32_rdy", "h_hi", "h_lo", "y_done", "ya_rdy",
                             "yb_rdy", "y_rdy", "z_st")]
        sexp_rdy, srec_rdy, high_rdy, zi_rdy, wd_rdy, wf_rdy, wn_rdy, wt_rdy = [
            sem(s) for s in ("sexp_rdy", "srec_rdy", "high_rdy", "zi_rdy",
                             "wd_rdy", "wf_rdy", "wn_rdy", "wt_rdy")]
        LOOPED = (TILES - 3) // 2

        def tiles(eng, body):
            for t in range(4):
                body(t, t % 2, t // 2)
            with eng.Fori(2, LOOPED) as q:
                for s in range(2):
                    body(2 * q + s, s, q)
            for t in range(2 * LOOPED, TILES):
                body(t, t % 2, t // 2)

        def there(t):
            return not isinstance(t, int) or 0 <= t < TILES

        h_ps = [tp[a // 2][:, 512 * (a % 2):512 * (a % 2) + 512] for a in range(4)]
        xT_ps = small[:, 0:D]
        b1_ps = acc[0][:, 0, 0:E * KH]

        with nc.Block() as block:

            @block.sync
            def _(sp):
                sp.dma_start(b2s.rearrange("p (a n) -> p a n", a=1),
                             b2.rearrange("(a e) d -> a (e d)", a=1).rearrange("a n -> a n")
                             .to_broadcast((P, E * D)).rearrange("p (a n) -> p a n", a=1)).then_inc(b2_ld, 16)
                sp.wait_ge(tables, 1)
                with sp.Fori(0, E) as e:
                    r0 = sp.value_load(padat[0:1, bass.ds(e, 1)], min_val=0, max_val=SPARE - P)
                    sp.dma_start(x_rows[bass.ds(r0, P), :], padrow[:, :]).then_inc(pad_st, 16)
                sp.wait_ge(pad_st, 16 * E)

                def body(t, s, q):
                    need(sp, xT_done, t - 1)
                    need(sp, wn_rdy, t - 1)
                    need(sp, zi_rdy, t - 1)
                    r0 = sp.value_load(base_i[0:1, bass.ds(t, 1)], min_val=0, max_val=XROWS - TOPK - P)
                    sp.dma_start(xr[:, s, :], x_rows[bass.ds(r0, P), :]).then_inc(xr_ld[s], 16)

                tiles(sp, body)
                sp.dma_start(x1_all[:, :, :], x1_rows.rearrange("(t p) d -> p t d", p=P)).then_inc(x1_ld, 16)

            @block.scalar
            def _(act):
                act.wait_ge(b1_done, 1)
                nc.scalar.activation(b1t[:, :], b1_ps, ACT.Copy, scale=S_H).then_inc(b1_rdy, 1)

                def x_hi(t, s):
                    act.wait_ge(xT_done, t + 1)
                    need(act, h_done, 2 * (t - 1))
                    nc.scalar.activation(xT[:, s, 0, :, :], xT_ps.rearrange("p (k n) -> p k n", k=KD), ACT.Copy,
                                         scale=S_X).then_inc(xT_hi, 1)

                def hidden_hi(t, s):
                    for a in range(2):
                        act.wait_ge(h32_rdy, 2 * t + a + 1)
                        need(act, y_done, t - 1)
                        nc.scalar.activation(hsp[:, s, 0, 4 * a:4 * a + 4, :],
                                             h32[:, a, :].rearrange("p (c n) -> p c n", c=4), ACT.Relu) \
                            .then_inc(h_hi, 1)

                def exps(t, s, q):
                    act.wait_ge(xr_ld[s], 16 * (q + 1))
                    need(act, srec_rdy, t - 1)
                    nc.scalar.activation(sexp[:, s, :], xr[:, s, C_SLO:C_SHI + 1], ACT.Exp, accum_out=ssum[:, s, :]) \
                        .then_inc(sexp_rdy, 1)

                def weigh(t, s):
                    act.wait_ge(yb_rdy, t + 1)
                    act.wait_ge(wt_rdy, t + 1)
                    need(act, z_st, 16 * (t - 1))
                    nc.scalar.activation(yrow[:, s, :], ysum[:, s, :], ACT.Copy, scale=wt[:, s, :]) \
                        .then_inc(y_rdy, 1)

                def body(t, s, q):
                    if there(t - 1):
                        weigh(t - 1, 1 - s)
                    if there(t + 2):
                        x_hi(t + 2, s)
                    if there(t + 1):
                        hidden_hi(t + 1, 1 - s)
                        exps(t + 1, 1 - s, q + s)

                x_hi(0, 0)
                x_hi(1, 1)
                exps(0, 0, 0)
                hidden_hi(0, 0)
                tiles(act, body)
                weigh(TILES - 1, (TILES - 1) % 2)

            @block.gpsimd
            def _(pool):
                pool.wait_ge(tables, 1)

                def gate_weights(t, s):
                    pool.wait_ge(high_rdy, t + 1)
                    need(pool, z_st, 16 * (t - 1))
                    hold(pool)
                    nc.gpsimd.tensor_scalar(zi[:, s, :], high[:, s, :], float(NP), xr[:, s, C_TOK:XW], ALU.mult,
                                            ALU.add).then_inc(zi_rdy, 1)
                    pool.wait_ge(sexp_rdy, t + 1)
                    nc.gpsimd.tensor_tensor(wd[:, s, :], sexp[:, s, 1:2], sexp[:, s, 0:1], ALU.subtract) \
                        .then_inc(wd_rdy, 1)
                    pool.wait_ge(wd_rdy, t + 1)
                    nc.gpsimd.tensor_tensor(wf[:, s, :], wd[:, s, :], high[:, s, :], ALU.mult).then_inc(wf_rdy, 1)
                    pool.wait_ge(wf_rdy, t + 1)
                    need(pool, wt_rdy, t - 1)
                    nc.gpsimd.tensor_tensor(wn[:, s, :], wf[:, s, :], sexp[:, s, 0:1], ALU.add).then_inc(wn_rdy, 1)

                def scatter(t, s):
                    pool.wait_ge(y_rdy, t + 1)
                    pool.wait_ge(zi_rdy, t + 1)
                    need(pool, z_st, 16 * t)
                    hold(pool)
                    nc.gpsimd.indirect_dma_start(
                        out=z_rows, out_offset=bass.IndirectOffsetOnAxis(ap=zi[:, s, :].bitcast(u32), axis=0),
                        in_=yrow[:, s, :], in_offset=None).then_inc(z_st, 16)

                def body(t, s, q):
                    if there(t - 1):
                        scatter(t - 1, 1 - s)
                    if there(t + 1):
                        gate_weights(t + 1, 1 - s)

                gate_weights(0, 0)
                tiles(pool, body)
                scatter(TILES - 1, (TILES - 1) % 2)
                pool.wait_ge(z_st, 16 * TILES)

            @block.vector
            def _(dve):
                steps = [0]

                def step(ins):
                    steps[0] += 1
                    ins.then_inc(tstep, 1)
                    dve.wait_ge(tstep, steps[0])

                def over(ap, n, pattern):
                    return ap.rearrange(pattern, **{"z": 1}).to_broadcast(n)

                step(nc.vector.tensor_scalar(thr[:, :], iota_t[:, 0:NT], float(P), None, ALU.mult))
                step(nc.vector.memset(one_e[:, :], 1.0))
                dve.wait_ge(total_done, 1)
                step(nc.vector.tensor_tensor(cmp_n, over(total_ps, (P, E, NT), "p (e z) -> p e z"),
                                             over(thr[:, :], (P, E, NT), "p (z k) -> p z k"), ALU.is_gt))
                step(nc.vector.tensor_reduce(filled[:, :], cmp_n, axis=AX.X, op=ALU.add))
                step(nc.vector.tensor_tensor_scan(cum[:, :], one_e[:, :], filled[:, :], 0.0, ALU.mult, ALU.add))
                step(nc.vector.tensor_tensor(cmp_t, over(iota_t[:, :], (P, TILES, E), "p (t z) -> p t z"),
                                             over(cum[:, :], (P, TILES, E), "p (z e) -> p z e"), ALU.is_ge))
                step(nc.vector.tensor_reduce(e_raw, cmp_t, axis=AX.X, op=ALU.add))
                step(nc.vector.tensor_tensor(cmp_w, cmp_t, over(filled[:, :], (P, TILES, E), "p (z e) -> p z e"),
                                             ALU.mult))
                step(nc.vector.tensor_reduce(start_t, cmp_w, axis=AX.X, op=ALU.add))
                step(nc.vector.tensor_tensor(start_t, iota_t[:, :], start_t, ALU.subtract))
                step(nc.vector.tensor_scalar(base_f, e_raw, float(CAP), None, ALU.mult))
                step(nc.vector.scalar_tensor_tensor(base_i[:, :], start_t, float(P), base_f, ALU.mult,
                                                    ALU.add))
                step(nc.vector.tensor_scalar(e_f[:, :], e_raw, float(E - 1), None, ALU.min))
                step(nc.vector.tensor_copy(e_i[:, :], e_f[:, :]))
                nc.vector.tensor_tensor(padat[:, :], total_ps, region[:, :], ALU.add).then_inc(tables, 1)
                dve.wait_ge(tables, 1)

                def x_lo(t, s):
                    dve.wait_ge(xT_hi, t + 1)
                    nc.vector.scalar_tensor_tensor(xT[:, s, 1, :, :], xT_ps.rearrange("p (k n) -> p k n", k=KD), S_X,
                                                   xT[:, s, 0, :, :], ALU.mult, ALU.subtract).then_inc(xT_lo, 1)

                def which(t, s, q):
                    dve.wait_ge(xr_ld[s], 16 * (q + 1))
                    need(dve, zi_rdy, t - 1)
                    need(dve, wf_rdy, t - 1)
                    nc.vector.tensor_scalar(high[:, s, :], xr[:, s, C_ELO:C_ELO + 1], e_f[:, bass.ds(t, 1)], None,
                                            ALU.is_lt).then_inc(high_rdy, 1)

                def hidden(t, s):
                    e = dve.value_load(e_i[0:1, bass.ds(t, 1)], min_val=0, max_val=E - 1)
                    for a in range(2):
                        dve.wait_ge(h_done, 2 * t + a + 1)
                        need(dve, h_lo, 2 * t - 1 + a)
                        nc.vector.scalar_tensor_tensor(
                            h32[:, a, :].rearrange("p (c n) -> p c n", c=4),
                            h_ps[2 * s + a].rearrange("p (c n) -> p c n", c=4), S_H / (S_X * S_W),
                            b1t[:, bass.ds(e * KH + 4 * a, 4)].rearrange("p (c z) -> p c z", z=1)
                            .to_broadcast((P, 4, P)), ALU.mult, ALU.add).then_inc(h32_rdy, 1)
                    for a in range(2):
                        dve.wait_ge(h_hi, 2 * t + a + 1)
                        nc.vector.scalar_tensor_tensor(
                            hsp[:, s, 1, 4 * a:4 * a + 4, :], h32[:, a, :].rearrange("p (c n) -> p c n", c=4), 0.0,
                            hsp[:, s, 0, 4 * a:4 * a + 4, :], ALU.max, ALU.subtract).then_inc(h_lo, 1)

                def result(t, s):
                    dve.wait_ge(sexp_rdy, t + 1)
                    nc.vector.reciprocal(srec[:, s, :], ssum[:, s, :]).then_inc(srec_rdy, 1)
                    dve.wait_ge(srec_rdy, t + 1)
                    dve.wait_ge(wn_rdy, t + 1)
                    need(dve, y_rdy, t - 1)
                    nc.vector.tensor_tensor(wt[:, s, :], wn[:, s, :], srec[:, s, :], ALU.mult).then_inc(wt_rdy, 1)
                    e = dve.value_load(e_i[0:1, bass.ds(t, 1)], min_val=0, max_val=E - 1)
                    dve.wait_ge(y_done, t + 1)
                    nc.vector.scalar_tensor_tensor(ysum[:, s, :], acc[s][:, 0, :], 1.0 / (S_H * S_W),
                                                   b2s[:, bass.ds(e * D, D)], ALU.mult, ALU.add) \
                        .then_inc(ya_rdy, 1)
                    dve.wait_ge(ya_rdy, t + 1)
                    nc.vector.scalar_tensor_tensor(ysum[:, s, :], acc[s][:, 1, :], 1.0 / (S_H * S_W), ysum[:, s, :],
                                                   ALU.mult, ALU.add).then_inc(yb_rdy, 1)

                def body(t, s, q):
                    if there(t - 1):
                        result(t - 1, 1 - s)
                    if there(t + 2):
                        x_lo(t + 2, s)
                    if there(t + 1):
                        which(t + 1, 1 - s, q + s)
                        hidden(t + 1, 1 - s)

                which(0, 0, 0)
                x_lo(0, 0)
                x_lo(1, 1)
                dve.wait_ge(b1_rdy, 1)
                dve.wait_ge(b2_ld, 16)
                hidden(0, 0)
                tiles(dve, body)
                result(TILES - 1, (TILES - 1) % 2)

            @block.tensor
            def _(pe):
                nc.tensor.matmul(total_ps, ones[:, :], count[:, NT % 2, :], start=True, stop=True) \
                    .then_inc(total_done, 1)
                nc.tensor.transpose(b1_ps, b1r[:, :], ident[0:E * KH, 0:E * KH]).then_inc(b1_done, 1)
                pe.wait_ge(tables, 1)

                def turn(t, s, q):
                    pe.wait_ge(xr_ld[s], 16 * (q + 1))
                    need(pe, xT_lo, t)
                    for k in range(KD):
                        last = nc.tensor.transpose(xT_ps[:, k * P:(k + 1) * P], xr[:, s, k * P:(k + 1) * P],
                                                   ident[:, :])
                    last.then_inc(xT_done, 1)

                def up(t, s):
                    e = pe.value_load(e_i[0:1, bass.ds(t, 1)], min_val=0, max_val=E - 1)
                    pe.wait_ge(xT_lo, t + 1)
                    need(pe, h32_rdy, 2 * (t - 1))
                    for c in range(KH):
                        for k in range(KD):
                            for n, (wv, xv) in enumerate(((0, 0), (0, 1), (1, 0))):
                                w = w1s[:, bass.ds(e, 1), wv, k, c * P:(c + 1) * P].rearrange("p a n -> p (a n)")
                                last = nc.tensor.matmul(h_ps[2 * s + c // 4][:, c % 4 * P:(c % 4 + 1) * P], w,
                                                        xT[:, s, xv, k, :], start=(k == 0 and n == 0),
                                                        stop=(k == KD - 1 and n == 2))
                        if c % 4 == 3:
                            last.then_inc(h_done, 1)

                def down(t, s):
                    e = pe.value_load(e_i[0:1, bass.ds(t, 1)], min_val=0, max_val=E - 1)
                    need(pe, yb_rdy, t - 1)
                    for c in range(KH):
                        if c % 4 == 0:
                            pe.wait_ge(h_lo, 2 * t + c // 4 + 1)
                        w = w2s[:, bass.ds(e, 1), c, :, :].rearrange("p a v d -> p (a v) d")
                        nc.tensor.matmul(acc[s][:, :, :], hsp[:, s, 0, c, :], w, start=(c == 0), stop=False,
                                         skip_group_check=True)
                        last = nc.tensor.matmul(acc[s][:, 1, :], hsp[:, s, 1, c, :], w[:, 0, :], start=False,
                                                stop=(c == KH - 1), skip_group_check=True)
                    last.then_inc(y_done, 1)

                def body(t, s, q):
                    if there(t + 2):
                        turn(t + 2, s, q + 1)
                    if there(t + 1):
                        up(t + 1, 1 - s)
                    down(t, s)

                pe.wait_ge(b1_rdy, 1)
                turn(0, 0, 0)
                turn(1, 1, 0)
                up(0, 0)
                tiles(pe, body)

        CT = 5
        chunks = [(c, min(CT, NT - 1 - c)) for c in range(0, NT - 1, CT)] + [(NT - 1, 1)]
        z_all = w1s[:, :, :, :, :].rearrange("p e v k h -> p (e v k h)").bitcast(f32)[:, 0:2 * NT * D] \
            .rearrange("p (c t d) -> p c t d", c=2, t=NT)
        z_ld = [sem(f"z_ld{i}") for i in range(len(chunks))]
        low_added, all_added, out_st = sem("low_added"), sem("all_added"), sem("out_st")

        with nc.Block() as block:

            @block.sync
            def _(sp):
                for n, (c0, nt) in enumerate(chunks):
                    for c in range(2):
                        r0 = c * NP + c0 * P
                        if c0 < NT - 1:
                            sp.dma_start(z_all[:, c, c0:c0 + nt, :], z_rows[r0:r0 + nt * P, :]
                                         .rearrange("(t p) d -> p t d", p=P)).then_inc(z_ld[n], 16)
                        else:
                            sp.dma_start(z_all[0:LAST16, c, c0, :], z_rows[r0:r0 + LAST16, :]).then_inc(z_ld[n], 16)
                            sp.dma_start(z_all[LAST16:LAST, c, c0, :], z_rows[r0 + LAST16:r0 + LAST, :]) \
                                .then_inc(z_ld[n], 16)

            @block.vector
            def _(dve):
                dve.wait_ge(x1_ld, 16)
                for n, (c0, nt) in enumerate(chunks):
                    rows, sems = (P, 2) if c0 < NT - 1 else (LAST, 4)
                    x1c = x1_all[0:rows, c0:c0 + nt, :]
                    dve.wait_ge(z_ld[n], 16 * sems)
                    nc.vector.tensor_tensor(x1c, x1c, z_all[0:rows, 0, c0:c0 + nt, :], ALU.add) \
                        .then_inc(low_added, 1)
                    dve.wait_ge(low_added, n + 1)
                    nc.vector.tensor_tensor(x1c, x1c, z_all[0:rows, 1, c0:c0 + nt, :], ALU.add) \
                        .then_inc(all_added, 1)

            @block.scalar
            def _(act):
                for n, (c0, nt) in enumerate(chunks):
                    act.wait_ge(all_added, n + 1)
                    if c0 < NT - 1:
                        act.dma_start(out[c0 * P:(c0 + nt) * P, :].rearrange("(t p) d -> p t d", p=P),
                                      x1_all[:, c0:c0 + nt, :]).then_inc(out_st, 16)
                    else:
                        act.dma_start(out[c0 * P:c0 * P + LAST16, :], x1_all[0:LAST16, c0, :]).then_inc(out_st, 16)
                        act.dma_start(out[c0 * P + LAST16:N, :], x1_all[LAST16:LAST, c0, :]).then_inc(out_st, 16)
                act.wait_ge(out_st, 16 * (len(chunks) + 1))


_INS = ["x", "adj", "L0_gnn_W", "L0_ffn_W1", "L0_ffn_b1", "L0_ffn_W2", "L0_ffn_b2", "L0_ffn_Wg", "L0_ffn_bg"]
_OUTS = [((N, D), "float32")]


def kernel(**inputs):
    import numpy as _np
    import concourse.bacc as _bacc
    from concourse import mybir as _mybir
    from concourse.bass_utils import run_bass_kernel_spmd as _run

    nc = _bacc.Bacc("TRN2", target_bir_lowering=False, num_devices=1)
    arrays, args = {}, []
    for name in _INS:
        a = _np.ascontiguousarray(inputs[name])
        arrays[f"in_{name}_dram"] = a
        args.append(nc.dram_tensor(f"in_{name}_dram", a.shape, _mybir.dt.from_np(a.dtype), kind="ExternalInput").ap())
    for i, (shape, dtype) in enumerate(_OUTS):
        dt = _mybir.dt.from_np(_np.dtype(dtype))
        args.append(nc.dram_tensor(f"out_{i}_dram", shape, dt, kind="ExternalOutput").ap())
    gnn_moe(nc, *args)
    r = _run(nc, [arrays], core_ids=[0])
    return r.results[0]["out_0_dram"]
```

```python
import concourse.bass as bass
from concourse import mybir
from contextlib import ExitStack


f32 = mybir.dt.float32
f16 = mybir.dt.float16
bf16 = mybir.dt.bfloat16
i32 = mybir.dt.int32
u32 = mybir.dt.uint32
ALU = mybir.AluOpType
ACT = mybir.ActivationFunctionType
AX = mybir.AxisListType

P = 128
N = 3327
D = 256
H = 1024
E = 8
TOPK = 2
EPS = 1e-5
NT = (N + P - 1) // P
NP = NT * P
LAST = N - (NT - 1) * P
LAST16 = LAST // 16 * 16
KD = D // P
KH = H // P

GROUPS = [(0, 5), (5, 5), (10, 4), (14, 4), (18, 4), (22, 4)]
NG = len(GROUPS)
GW = 5 * P
NBUF = 3
AHEAD = 2
PAIRS = NT // 2

S_ADJ = 2.0 ** 6
S_HID = 2.0 ** 4
S_W = 2.0 ** 8
S_X = 2.0 ** 5
S_H = 2.0 ** 4

NH = 2
S = NH * P
TILES = (TOPK * N + E * (S - 1)) // S
LEAST = (TOPK * N + S - 1) // S
CAP = (N + S - 1) // S * S + S
SPARE = E * CAP
DUMP = SPARE + (TILES - LEAST) * S
XROWS = DUMP + TOPK
C_SLO, C_SHI, C_ELO, C_TOK, XW = D, D + 1, D + 2, D + 3, D + 4
SROWS = NP + S


def gnn_moe(nc, x, adj, gnn_w, w1, b1, w2, b2, wg, bg, out):
    ctx = ExitStack()
    with ctx:
        def sb(name, shape, dt):
            return ctx.enter_context(nc.sbuf_tensor(name, shape, dt))

        def pb(name, shape, dt=f32):
            return ctx.enter_context(nc.psum_tensor(name, shape, dt))

        def sem(name):
            return ctx.enter_context(nc.semaphore(name))

        x_rows = nc.dram_tensor("x_rows", [XROWS, XW], f32, kind="Internal").ap()
        sums = nc.dram_tensor("sums", [SROWS, D], f32, kind="Internal").ap()

        w1s = sb("w1s", [P, E, 2, KD, H], f16)
        w2s = sb("w2s", [P, E, KH, 2, D], f16)
        hid = sb("hid", [P, NT, 2, D], f16)
        adj_in = sb("adj_in", [P, 2, NP], f32)
        adjT = sb("adjT", [P, NBUF, 2, GW], f16)
        wst = sb("wst", [P, 2, H], f32)
        xin = sb("xin", [P, 2, D], f32)
        row = sb("row", [P, 2, XW], f32)
        padrow = sb("padrow", [P, NH, XW], f32)
        x1T = sb("x1T", [P, KD, P], f32)
        ident = sb("ident", [P, P], f32)
        before = sb("before", [P, P], bf16)
        ones = sb("ones", [P, P], bf16)
        wrow = sb("wrow", [P, D], f32)
        wgs = sb("wgs", [P, KD, E], f32)
        bgs = sb("bgs", [P, E], f32)
        b1r = sb("b1r", [E * KH, P], f32)
        b1t = sb("b1t", [P, E * KH], f32)
        stats = sb("stats", [P, 6], f32)
        mv = sb("mv", [P, 2], f32)
        sd = sb("sd", [P, 1], f32)
        rstd = sb("rstd", [P, 1], f32)
        iota_i = sb("iota_i", [P, TILES], i32)
        iota_e = sb("iota_e", [P, E], f32)
        iota_t = sb("iota_t", [P, TILES], f32)
        region = sb("region", [P, E], f32)
        tok_i = sb("tok_i", [P, NT], i32)
        tok = sb("tok", [P, NT], f32)
        live = sb("live", [P, NT], f32)
        dump = sb("dump", [P, NT, TOPK], f32)
        pad_i = sb("pad_i", [P, NH], i32)
        score = sb("score", [P, E], f32)
        top = sb("top", [P, E], f32)
        below = sb("below", [P, E], f32)
        topix = sb("topix", [P, E], u32)
        topf = sb("topf", [P, TOPK], f32)
        ehi = sb("ehi", [P, 1], f32)
        hot = sb("hot", [P, TOPK, E], f32)
        both = sb("both", [P, E], bf16)
        count = sb("count", [P, 2, E], bf16)
        place = sb("place", [P, E], f32)
        junk = sb("junk", [P, TOPK, E], f32)
        posf = sb("posf", [P, TOPK], f32)
        pos = sb("pos", [P, 2, TOPK], i32)
        epsc = sb("epsc", [P, 1], f32)
        x_all = w2s[:, E // 2:E].rearrange("p e k s d -> p (e k s d)").bitcast(f32)[:, 0:NT * D] \
            .rearrange("p (t d) -> p t d", t=NT)
        early = adjT[:, NBUF - 1, :, :].rearrange("p a b -> p (a b)").bitcast(f32)
        stats_x = early[:, 0:NT * 6].rearrange("p (t n) -> p t n", t=NT)
        mv_x = early[:, 160:160 + 2 * NT].rearrange("p (t n) -> p t n", t=NT)
        sd_x, rstd_x, shift_x = (early[:, 224 + 32 * n:224 + 32 * n + NT] for n in range(3))
        hid32 = wst[:, :, :].rearrange("p a (b d) -> p a b d", b=4)

        tp = [pb(f"tp{i}", [P, 1024]) for i in range(2)]
        acc = [pb(f"acc{i}", [P, 2, D]) for i in range(2)]
        small = pb("small", [P, 512])
        gate_ps = pb("gate_ps", [P, 512])
        scores_ps = gate_ps[:, 0:E]
        rank_ps = gate_ps[:, 128:128 + E]
        total_ps = gate_ps[:, 256:256 + E]

        const_set, const_ld = sem("const_set"), sem("const_ld")
        XCUT = [0, 5, 10, 15, 20, NT - 1]
        x_in = [sem(f"x_in{n}") for n in range(len(XCUT))]
        tail_zero = sem("tail_zero")
        norm1b = sem("norm1b")
        stats1, mv1, sd1, rstd1, shift1, norm1, hid32_rdy, hid_hi, hid_lo = [
            sem(s) for s in ("stats1", "mv1", "sd1", "rstd1", "shift1", "norm1", "hid32_rdy", "hid_hi", "hid_lo")]
        adj_ld = [sem(f"adj_ld{i}") for i in range(2)]
        tposed, adj_hi, adj_lo, mm_done = [sem(s) for s in ("tposed", "adj_hi", "adj_lo", "mm_done")]
        xin_ld = [sem(f"xin_ld{i}") for i in range(2)]
        x1_st = [sem(f"x1_st{i}") for i in range(2)]
        x1a, x1b, st2, mv2, sd2, rstd2, norm2, tok_rdy = [
            sem(s) for s in ("x1a", "x1b", "st2", "mv2", "sd2", "rstd2", "norm2", "tok_rdy")]
        nT_done, nT_rdy, gate_done = sem("nT_done"), sem("nT_rdy"), sem("gate_done")
        sc_rdy, top_rdy, below_rdy, ix_rdy, ixf_rdy, e_rdy, hot_rdy, both_rdy, slo_rdy, count_rdy = [
            sem(s) for s in ("sc_rdy", "top_rdy", "below_rdy", "ix_rdy", "ixf_rdy", "e_rdy", "hot_rdy", "both_rdy", "slo_rdy",
                             "count_rdy")]
        rank_done, place_rdy, posf_rdy, pos_rdy = [
            sem(s) for s in ("rank_done", "place_rdy", "posf_rdy", "pos_rdy")]
        sent = [sem(f"sent{i}") for i in range(2)]
        spare_st = sem("spare_st")
        w_ld = [sem(f"w_ld{i}") for i in range(2)]
        w_sc, w_hi, w_lo = sem("w_sc"), sem("w_hi"), sem("w_lo")

        def need(eng, s, v):
            if not isinstance(v, int) or v > 0:
                eng.wait_ge(s, v)

        def hold(eng):
            eng.nop(nofuse=True)

        HIDDEN_BY = []
        for g, (b0, nb) in enumerate(GROUPS):
            done = sum(len(x) for x in HIDDEN_BY)
            HIDDEN_BY.append(list(range(done, (b0 + nb + 1) // 2 + 1)))

        def pairs(eng, body):
            body(0, False)
            body(1, True)
            with eng.Fori(2, E + 1) as r:
                body(r, True)
            with eng.Fori(E + 1, PAIRS - 1) as r:
                body(r, False)
            body(PAIRS - 1, False)

        def load_rows(eng, dst, src, i, s):
            if isinstance(i, int) and i == NT - 1:
                eng.dma_start(dst[0:LAST16], src[i * P:i * P + LAST16, :]).then_inc(s, 16)
                eng.dma_start(dst[LAST16:LAST], src[i * P + LAST16:N, :]).then_inc(s, 16)
            else:
                eng.dma_start(dst, src[bass.ds(i * P, P), :]).then_inc(s, 16)

        def two(i):
            return 2 if isinstance(i, int) and i == NT - 1 else 1

        def words(region):
            return region.rearrange("p a b c -> p (a b c)").bitcast(f32)

        KB = KH // 2
        pool_f = words(hid[:, :, :, :])
        hsp = pool_f[:, 0:4096].bitcast(f16).rearrange("p (s v c n) -> p s v c n", s=2, v=2, c=KH)
        h32 = pool_f[:, 4096:5120].rearrange("p (a c n) -> p a c n", a=2, c=2)
        ysum = pool_f[:, 5120:5120 + NH * D].rearrange("p (h d) -> p h d", h=NH)
        b2t = pool_f[:, 5632:5632 + 2 * D].rearrange("p (s d) -> p s d", s=2)
        pool_t = adj_in[:, :, :].rearrange("p a b -> p (a b)")
        yrow = pool_t[:, 0:2 * NH * D].rearrange("p (s h d) -> p s h d", s=2, h=NH)
        xr = pool_t[:, 1024:1024 + 2 * NH * XW].rearrange("p (s h w) -> p s h w", s=2, h=NH)
        xT = pool_t[:, 2560:3584].bitcast(f16).rearrange("p (s v k n) -> p s v k n", s=2, v=2, k=KD)
        pool_w = wst[:, :, :].rearrange("p a b -> p (a b)")
        cmp_n = pool_w[:, 0:E * NT].rearrange("p (e k) -> p e k", e=E)
        cmp_t = pool_w[:, 512:512 + TILES * E].rearrange("p (t e) -> p t e", e=E)
        cmp_w = pool_w[:, 1024:1024 + TILES * E].rearrange("p (t e) -> p t e", e=E)
        e_raw, start_t, base_f = (pool_w[:, 1536 + 64 * i:1536 + 64 * i + TILES] for i in range(3))
        h_ps = [tp[a // 2][:, 512 * (a % 2):512 * (a % 2) + 512].rearrange("p (c n) -> p c n", c=2)
                for a in range(KB)]
        xT_ps = small[:, :].rearrange("p (k n) -> p k n", k=KD)
        b1_ps = acc[0][:, 0, 0:E * KH]
        N16 = N // 16 * 16

        KT = -(-N // S)
        thr = sb("thr", [P, KT], f32)
        one_e = sb("one_e", [P, E], f32)
        filled = sb("filled", [P, E], f32)
        cum = sb("cum", [P, E], f32)
        e_f = sb("e_f", [P, TILES], f32)
        e_i = sb("e_i", [P, TILES], i32)
        base_i = sb("base_i", [P, TILES], i32)
        padat = sb("padat", [P, E], i32)
        sexp = pool_w[:, 1792:1800].rearrange("p (s h c) -> p s h c", s=2, h=NH)
        ssum, srec, high, wd, wf, wn, wt = (
            pool_w[:, 1800 + 4 * n:1804 + 4 * n].rearrange("p (s h) -> p s h", s=2) for n in range(7))
        meta = pool_w[:, 1840:1840 + 2 * NH * (XW - D)].rearrange("p (s h w) -> p s h w", s=2, h=NH)
        zi = sb("zi", [P, 2, NH], i32)

        total_done, tstep, tables, b1_done, b1_rdy, pad_st, out_st = [
            sem(s) for s in ("total_done", "tstep", "tables", "b1_done", "b1_rdy", "pad_st", "out_st")]
        xr_ld = [sem(f"xr_ld{i}") for i in range(2)]
        b2_ld = [sem(f"b2_ld{i}") for i in range(2)]
        xT_done, xT_hi, xT_lo, h_done, h32_rdy, h_hi, h_lo, y_done, ya_rdy, yb_rdy, y_rdy, z_st = [
            sem(s) for s in ("xT_done", "xT_hi", "xT_lo", "h_done", "h32_rdy", "h_hi", "h_lo", "y_done", "ya_rdy",
                             "yb_rdy", "y_rdy", "z_st")]
        meta_rdy = sem("meta_rdy")
        sexp_rdy, ssum_rdy, srec_rdy, high_rdy, zi_rdy, wd_rdy, wf_rdy, wn_rdy, wt_rdy = [
            sem(s) for s in ("sexp_rdy", "ssum_rdy", "srec_rdy", "high_rdy", "zi_rdy", "wd_rdy", "wf_rdy",
                             "wn_rdy", "wt_rdy")]
        LOOPED = (TILES - 3) // 2

        def tiles(eng, body):
            for t in range(4):
                body(t, t % 2, t // 2)
            with eng.Fori(2, LOOPED) as q:
                for s in range(2):
                    body(2 * q + s, s, q)
            for t in range(2 * LOOPED, TILES):
                body(t, t % 2, t // 2)

        def there(t):
            return not isinstance(t, int) or 0 <= t < TILES

        with nc.Block() as block:

            @block.sync
            def _(sp):
                sp.wait_ge(tail_zero, 1)
                for n, (t0, t1) in enumerate(zip(XCUT, XCUT[1:])):
                    sp.dma_start(x_all[:, t0:t1, :],
                                 x[t0 * P:t1 * P, :].rearrange("(t p) d -> p t d", p=P)).then_inc(x_in[n], 16)
                load_rows(sp, x_all[:, NT - 1, :], x, NT - 1, x_in[-1])
                sp.dma_start(wrow[:, :], gnn_w.rearrange("(a d) -> a d", a=1).to_broadcast((P, D))) \
                    .then_inc(const_ld, 16)
                sp.dma_start(wgs[:, :, :], wg.rearrange("(k p) e -> p k e", p=P)).then_inc(const_ld, 16)
                sp.dma_start(bgs[:, :], bg.rearrange("(a e) -> a e", a=1).to_broadcast((P, E))) \
                    .then_inc(const_ld, 16)
                sp.dma_start(b1r[:, :], b1.rearrange("e (c p) -> (e c) p", p=P)).then_inc(const_ld, 16)

                def load_weights(e, u):
                    src = w1[bass.ds(e, 1), u * P:(u + 1) * P, :].rearrange("a p h -> p (a h)") if u < KD else \
                        w2[bass.ds(e, 1), (u - KD) * 4 * P:(u - KD + 1) * 4 * P, :] \
                        .rearrange("a (c p) d -> p (a c) d", p=P)
                    dst = wst[:, u % 2, :] if u < KD else wst[:, u % 2, :].rearrange("p (c d) -> p c d", c=4)
                    sp.dma_start(dst, src).then_inc(w_ld[u % 2], 16)

                def body(r, weights):
                    for s in range(2):
                        i = 2 * r + s
                        need(sp, tposed, NG * (i - 1))
                        load_rows(sp, adj_in[:, s, 0:N], adj, i, adj_ld[s])
                        if not (isinstance(i, int) and i < 2):
                            store_x1(i - 2, s)
                            sp.wait_ge(x1_st[s], 16 * r)
                            sp.wait_ge(norm2, i - 1)
                        load_rows(sp, xin[:, s, :], x, i, xin_ld[s])
                        if weights:
                            for u in (2 * s, 2 * s + 1):
                                sp.wait_ge(w_lo, 4 * r + u - 2 - 1)
                                load_weights(r - 1, u)

                def store_x1(i, s):
                    sp.wait_ge(x1b, i + 1)
                    sp.dma_start(sums[bass.ds(i * P, P), :], xin[:, s, :]).then_inc(x1_st[s], 16)

                pairs(sp, body)
                for s in range(2):
                    store_x1(NT - 2 + s, s)
                sp.wait_ge(tables, 1)
                with sp.Fori(0, E) as e:
                    r0 = sp.value_load(padat[0:1, bass.ds(e, 1)], min_val=0, max_val=SPARE - S)
                    sp.dma_start(x_rows[bass.ds(r0, S), :].rearrange("(h p) w -> p h w", p=P), padrow[:, :, :]) \
                        .then_inc(pad_st, 16)
                sp.wait_ge(pad_st, 16 * E)
                for s in range(2):
                    sp.wait_ge(x1_st[s], 16 * PAIRS)

            @block.scalar
            def _(act):
                act.wait_ge(const_set, 1)
                act.wait_ge(mv1, NT)
                nc.scalar.activation(sd_x, mv_x[:, :, 1], ACT.Sqrt, bias=epsc[:, :]).then_inc(sd1, 1)

                def norm_hidden(j):
                    act.wait_ge(shift1, 1)
                    need(act, hid_lo, j - 1)
                    nc.scalar.activation(hid32[:, j % 2, 0, :], x_all[:, 2 * j, :], ACT.Identity,
                                         bias=shift_x[:, 2 * j:2 * j + 1],
                                         scale=rstd_x[:, 2 * j:2 * j + 1]).then_inc(norm1, 1)

                def hi_hidden(j):
                    act.wait_ge(hid32_rdy, j + 1)
                    nc.scalar.activation(hid[:, 2 * j:2 * j + 2, 0, :], hid32[:, j % 2, 2:4, :], ACT.Copy,
                                         scale=S_HID).then_inc(hid_hi, 1)

                def hidden_pair(j):
                    if j < PAIRS:
                        norm_hidden(j)
                    if j:
                        hi_hidden(j - 1)

                def body(r, weights):
                    for s in range(2):
                        i = 2 * r + s
                        for g, (b0, nb) in enumerate(GROUPS):
                            n = NG * i + g
                            if isinstance(i, int) and i == 0:
                                for j in HIDDEN_BY[g]:
                                    hidden_pair(j)
                            act.wait_ge(tposed, n + 1)
                            need(act, mm_done, n - NBUF + 1)
                            nc.scalar.activation(adjT[:, g % NBUF, 0, 0:nb * P], tp[g % 2][:, 0:nb * P],
                                                 ACT.Copy, scale=S_ADJ).then_inc(adj_hi, 1)
                            if g == 2 and not (isinstance(i, int) and i == 0):
                                root(i - 1, 1 - s)
                            if g == 5 and not (isinstance(i, int) and i == 0):
                                gate_in(i - 1)
                            if weights and g in (1, 4):
                                split(r - 1, 2 * s + (g == 4))

                def root(i, s):
                    act.wait_ge(mv2, i + 1)
                    nc.scalar.activation(sd[:, :], mv[:, 1:2], ACT.Sqrt, bias=epsc[:, :]).then_inc(sd2, 1)

                def gate_in(i):
                    act.wait_ge(nT_done, i + 1)
                    need(act, gate_done, i)
                    nc.scalar.activation(x1T[:, :, :], small[:, 0:D].rearrange("p (k n) -> p k n", k=KD),
                                         ACT.Copy).then_inc(nT_rdy, 1)

                def split(e, u):
                    unit = 4 * e + u
                    act.wait_ge(w_ld[u % 2], 32 * e + 16 * (u // 2) + 16)
                    nc.scalar.activation(wst[:, u % 2, :], wst[:, u % 2, :], ACT.Copy, scale=S_W).then_inc(w_sc, 1)
                    act.wait_ge(w_sc, unit + 1)
                    dst = w1s[:, bass.ds(e, 1), 0, u, :].rearrange("p a h -> p (a h)") if u < KD else \
                        w2s[:, bass.ds(e, 1), (u - KD) * 4:(u - KD) * 4 + 4, 0, :].rearrange("p a c d -> p (a c) d")
                    src = wst[:, u % 2, :] if u < KD else wst[:, u % 2, :].rearrange("p (c d) -> p c d", c=4)
                    nc.scalar.activation(dst, src, ACT.Copy).then_inc(w_hi, 1)

                pairs(act, body)
                root(NT - 1, 1)
                gate_in(NT - 1)

            @block.gpsimd
            def _(pool):
                nc.gpsimd.memset(x_all[96:P, NT - 1, :], 0.0).then_inc(tail_zero, 1)
                pool.wait_ge(tail_zero, 1)
                nc.gpsimd.memset(epsc[:, :], EPS).then_inc(const_set, 1)
                nc.gpsimd.memset(adj_in[:, :, N:NP], 0.0)
                nc.gpsimd.memset(ident[:, :], 0.0)
                nc.gpsimd.memset(before[:, :], 0.0)
                nc.gpsimd.memset(ones[:, :], 1.0)
                nc.gpsimd.memset(live[:, :], 1.0)
                nc.gpsimd.memset(dump[:, :, :], 0.0)
                nc.gpsimd.memset(padrow[:, :, :], 0.0)
                nc.gpsimd.memset(count[:, 0, :], 0.0)
                nc.gpsimd.iota(iota_i[:, :], [[1, TILES]], base=0, channel_multiplier=0)
                nc.gpsimd.iota(tok_i[:, :], [[P, NT]], base=0, channel_multiplier=1)
                nc.gpsimd.iota(pad_i[:, :], [[P, NH]], base=NP, channel_multiplier=1).then_inc(const_set, 1)
                pool.wait_ge(const_set, 2)
                nc.gpsimd.affine_select(out=ident[:, :], in_=ident[:, :], compare_op=ALU.not_equal, fill=1.0,
                                        base=0, pattern=[[-1, P]], channel_multiplier=1)
                nc.gpsimd.affine_select(out=before[:, :], in_=before[:, :], compare_op=ALU.is_ge, fill=1.0,
                                        base=0, pattern=[[-1, P]], channel_multiplier=1)
                end = (NT - 1) * P + LAST
                nc.gpsimd.affine_select(out=live[:, :], in_=live[:, :], compare_op=ALU.not_equal, fill=0.0,
                                        base=-end, pattern=[[P, NT]], channel_multiplier=1)
                for c in range(TOPK):
                    nc.gpsimd.affine_select(out=dump[:, :, c], in_=dump[:, :, c], compare_op=ALU.not_equal,
                                            fill=float(DUMP + c), base=-end, pattern=[[P, NT]],
                                            channel_multiplier=1)
                nc.gpsimd.tensor_copy(iota_e[:, :], iota_i[:, 0:E])
                nc.gpsimd.tensor_copy(iota_t[:, :], iota_i[:, :])
                nc.gpsimd.tensor_copy(tok[:, :], tok_i[:, :])
                nc.gpsimd.tensor_scalar(region[:, :], iota_i[:, 0:E], float(CAP), None, ALU.mult)
                nc.gpsimd.tensor_copy(padrow[:, :, C_TOK], pad_i[:, :]).then_inc(const_set, 1)
                for j in range(PAIRS):
                    k = j % 2
                    pool.wait_ge(const_ld, 64)
                    pool.wait_ge(norm1, j + 1)
                    pool.wait_ge(norm1b, j + 1)
                    need(pool, hid_lo, j - 1)
                    nc.gpsimd.tensor_tensor(hid32[:, k, 2:4, :], hid32[:, k, 0:2, :],
                                            wrow[:, :].rearrange("p (a d) -> p a d", a=1).to_broadcast((P, 2, D)),
                                            ALU.mult).then_inc(hid32_rdy, 1)
                pool.wait_ge(const_set, 3)
                for c in range(TILES - LEAST):
                    pool.dma_start(x_rows[SPARE + c * S:SPARE + (c + 1) * S, :].rearrange("(h p) w -> p h w", p=P),
                                   padrow[:, :, :]).then_inc(spare_st, 16)
                pool.dma_start(sums[NP:NP + S, :].rearrange("(h p) d -> p h d", p=P),
                               padrow[:, :, 0:D]).then_inc(spare_st, 16)
                pool.wait_ge(hid_lo, PAIRS)
                pool.sem_inc(w_lo, 2)

                def body(r, weights):
                    for s in range(2):
                        i = 2 * r + s
                        for u in ((2 * s, 2 * s + 1) if weights else ()):
                            e = r - 1
                            pool.wait_ge(w_hi, 4 * e + u + 1)
                            src = wst[:, u % 2, :] if u < KD else \
                                wst[:, u % 2, :].rearrange("p (c d) -> p c d", c=4)
                            if u < KD:
                                hi, lo = (w1s[:, bass.ds(e, 1), a, u, :].rearrange("p a h -> p (a h)")
                                          for a in range(2))
                            else:
                                c = (u - KD) * 4
                                hi, lo = (w2s[:, bass.ds(e, 1), c:c + 4, a, :].rearrange("p a c d -> p (a c) d")
                                          for a in range(2))
                            nc.gpsimd.tensor_tensor(lo, src, hi, ALU.subtract).then_inc(w_lo, 1)
                        if not (isinstance(i, int) and i < 2):
                            dispatch(i - 2, s)

                def dispatch(i, s):
                    pool.wait_ge(pos_rdy, i + 1)
                    for c in range(TOPK):
                        hold(pool)
                        nc.gpsimd.indirect_dma_start(
                            out=x_rows, out_offset=bass.IndirectOffsetOnAxis(ap=pos[:, s, c:c + 1].bitcast(u32), axis=0),
                            in_=row[:, s, :], in_offset=None).then_inc(sent[s], 16)

                pairs(pool, body)
                dispatch(NT - 2, 0)
                dispatch(NT - 1, 1)
                pool.wait_ge(spare_st, 16 * (TILES - LEAST + 1))
                for s in range(2):
                    pool.wait_ge(sent[s], 16 * NT)

            def lo_hidden(dve, j):
                dve.wait_ge(hid_hi, j + 1)
                nc.vector.scalar_tensor_tensor(hid[:, 2 * j:2 * j + 2, 1, :], hid32[:, j % 2, 2:4, :], S_HID,
                                               hid[:, 2 * j:2 * j + 2, 0, :], ALU.mult, ALU.subtract) \
                    .then_inc(hid_lo, 1)

            def slot_tables(dve):
                steps = [0]

                def step(ins):
                    steps[0] += 1
                    ins.then_inc(tstep, 1)
                    dve.wait_ge(tstep, steps[0])

                def over(ap, n, pattern):
                    return ap.rearrange(pattern, **{"z": 1}).to_broadcast(n)

                dve.wait_ge(w_lo, 2 + 4 * E)
                step(nc.vector.tensor_scalar(thr[:, :], iota_t[:, 0:KT], float(S), None, ALU.mult))
                step(nc.vector.memset(one_e[:, :], 1.0))
                dve.wait_ge(total_done, 1)
                nc.vector.tensor_tensor(padat[:, :], total_ps, region[:, :], ALU.add).then_inc(tables, 1)
                counts = cmp_n[:, :, 0:KT]
                step(nc.vector.tensor_tensor(counts, over(total_ps, (P, E, KT), "p (e z) -> p e z"),
                                             over(thr[:, :], (P, E, KT), "p (z k) -> p z k"), ALU.is_gt))
                step(nc.vector.tensor_reduce(filled[:, :], counts, axis=AX.X, op=ALU.add))
                step(nc.vector.tensor_tensor_scan(cum[:, :], one_e[:, :], filled[:, :], 0.0, ALU.mult, ALU.add))
                step(nc.vector.tensor_tensor(cmp_t, over(iota_t[:, :], (P, TILES, E), "p (t z) -> p t z"),
                                             over(cum[:, :], (P, TILES, E), "p (z e) -> p z e"), ALU.is_ge))
                step(nc.vector.tensor_reduce(e_raw, cmp_t, axis=AX.X, op=ALU.add))
                step(nc.vector.tensor_tensor(cmp_w, cmp_t, over(filled[:, :], (P, TILES, E), "p (z e) -> p z e"),
                                             ALU.mult))
                step(nc.vector.tensor_reduce(start_t, cmp_w, axis=AX.X, op=ALU.add))
                step(nc.vector.tensor_tensor(start_t, iota_t[:, :], start_t, ALU.subtract))
                step(nc.vector.tensor_scalar(base_f, e_raw, float(CAP), None, ALU.mult))
                step(nc.vector.scalar_tensor_tensor(base_i[:, :], start_t, float(S), base_f, ALU.mult, ALU.add))
                step(nc.vector.tensor_scalar(e_f[:, :], e_raw, float(E - 1), None, ALU.min))
                step(nc.vector.tensor_copy(e_i[:, :], e_f[:, :]))

            @block.vector
            def _(dve):
                for t in range(NT):
                    if t in XCUT:
                        dve.wait_ge(x_in[XCUT.index(t)], 16 if t < NT - 1 else 32)
                    nc.vector.bn_stats(stats_x[:, t, :], x_all[:, t, :]).then_inc(stats1, 1)
                    if t:
                        dve.wait_ge(stats1, t)
                        nc.vector.bn_aggr(mv_x[:, t - 1, :], stats_x[:, t - 1, :]).then_inc(mv1, 1)
                dve.wait_ge(stats1, NT)
                nc.vector.bn_aggr(mv_x[:, NT - 1, :], stats_x[:, NT - 1, :]).then_inc(mv1, 1)
                dve.wait_ge(sd1, 1)
                nc.vector.reciprocal(rstd_x, sd_x).then_inc(rstd1, 1)
                dve.wait_ge(rstd1, 1)
                nc.vector.scalar_tensor_tensor(shift_x, mv_x[:, :, 0], -1.0, rstd_x, ALU.mult, ALU.mult) \
                    .then_inc(shift1, 1)

                def norm_hidden(j):
                    dve.wait_ge(shift1, 1)
                    need(dve, hid_hi, j - 1)
                    t = 2 * j + 1
                    nc.vector.tensor_scalar(hid32[:, j % 2, 1, :], x_all[:, t, :], rstd_x[:, t:t + 1],
                                            shift_x[:, t:t + 1], ALU.mult, ALU.add).then_inc(norm1b, 1)

                def hidden_pair(j):
                    if j < PAIRS:
                        norm_hidden(j)
                    if j:
                        lo_hidden(dve, j - 1)

                def body(r, weights):
                    for s in range(2):
                        i = 2 * r + s
                        first = isinstance(i, int) and i == 0
                        second = isinstance(i, int) and i < 2
                        for g, (b0, nb) in enumerate(GROUPS):
                            n = NG * i + g
                            if first:
                                for j in HIDDEN_BY[g]:
                                    hidden_pair(j)
                            dve.wait_ge(adj_hi, n + 1)
                            nc.vector.scalar_tensor_tensor(adjT[:, g % NBUF, 1, 0:nb * P], tp[g % 2][:, 0:nb * P],
                                                           S_ADJ, adjT[:, g % NBUF, 0, 0:nb * P], ALU.mult,
                                                           ALU.subtract).then_inc(adj_lo, 1)
                            if g == 1 and not second:
                                choose(i - 2, s)
                            if g == 1 and not first:
                                residual(i - 1, 1 - s, r if s else r - 1)
                            if g == 3 and not first:
                                normalise(i - 1, 1 - s, r if s else r - 1)
                            if g == 4 and not second:
                                positions(i - 2, s)

                def residual(i, s, turn):
                    dve.wait_ge(mm_done, NG * (i + 1))
                    dve.wait_ge(xin_ld[s], 16 * turn + 16 * two(i))
                    scale = 1.0 / (S_ADJ * S_HID)
                    nc.vector.scalar_tensor_tensor(xin[:, s, :], acc[s][:, 0, :], scale, xin[:, s, :], ALU.mult,
                                                   ALU.add).then_inc(x1a, 1)
                    dve.wait_ge(x1a, i + 1)
                    nc.vector.scalar_tensor_tensor(xin[:, s, :], acc[s][:, 1, :], scale, xin[:, s, :], ALU.mult,
                                                   ALU.add).then_inc(x1b, 1)
                    dve.wait_ge(x1b, i + 1)
                    nc.vector.bn_stats(stats[:, :], xin[:, s, :]).then_inc(st2, 1)
                    dve.wait_ge(st2, i + 1)
                    hold(dve)
                    nc.vector.bn_aggr(mv[:, :], stats[:, :]).then_inc(mv2, 1)

                def normalise(i, s, turn):
                    dve.wait_ge(sd2, i + 1)
                    nc.vector.reciprocal(rstd[:, :], sd[:, :]).then_inc(rstd2, 1)
                    dve.wait_ge(rstd2, i + 1)
                    need(dve, sent[s], 32 * turn)
                    nc.vector.tensor_scalar(row[:, s, 0:D], xin[:, s, :], mv[:, 0:1], rstd[:, :], ALU.subtract,
                                            ALU.mult).then_inc(norm2, 1)
                    nc.vector.tensor_copy(row[:, s, C_TOK:XW], tok[:, bass.ds(i, 1)]).then_inc(tok_rdy, 1)

                def choose(i, s):
                    dve.wait_ge(gate_done, i + 1)
                    nc.vector.tensor_tensor(score[:, :], scores_ps, bgs[:, :], ALU.add).then_inc(sc_rdy, 1)
                    dve.wait_ge(sc_rdy, i + 1)
                    hold(dve)
                    nc.vector.max(top[:, :], score[:, :]).then_inc(top_rdy, 1)
                    dve.wait_ge(top_rdy, i + 1)
                    nc.vector.tensor_scalar(below[:, :], score[:, :], top[:, 0:1], None, ALU.subtract) \
                        .then_inc(below_rdy, 1)
                    nc.vector.max_index(topix[:, :], top[:, :], score[:, :]).then_inc(ix_rdy, 1)
                    dve.wait_ge(ix_rdy, i + 1)
                    nc.vector.tensor_copy(topf[:, :], topix[:, 0:TOPK]).then_inc(ixf_rdy, 1)
                    dve.wait_ge(ixf_rdy, i + 1)
                    nc.vector.tensor_tensor(row[:, s, C_ELO:C_ELO + 1], topf[:, 0:1], topf[:, 1:2], ALU.min) \
                        .then_inc(e_rdy, 1)
                    nc.vector.tensor_tensor(ehi[:, :], topf[:, 0:1], topf[:, 1:2], ALU.max).then_inc(e_rdy, 1)
                    dve.wait_ge(e_rdy, 2 * i + 2)
                    for c, which in enumerate((row[:, s, C_ELO:C_ELO + 1], ehi[:, :])):
                        nc.vector.tensor_scalar(hot[:, c, :], iota_e[:, :], which, live[:, bass.ds(i, 1)],
                                                ALU.is_equal, ALU.mult).then_inc(hot_rdy, 1)
                    dve.wait_ge(hot_rdy, 2 * i + 2)
                    nc.vector.tensor_tensor(both[:, :], hot[:, 0, :], hot[:, 1, :], ALU.add).then_inc(both_rdy, 1)
                    dve.wait_ge(below_rdy, i + 1)
                    for c in range(TOPK):
                        nc.vector.scalar_tensor_tensor(junk[:, c, :], hot[:, c, :], 1.0, below[:, :], ALU.mult,
                                                       ALU.mult, accum_out=row[:, s, C_SLO + c:C_SLO + c + 1]) \
                            .then_inc(slo_rdy, 1)
                    dve.wait_ge(both_rdy, i + 1)
                    nc.vector.tensor_tensor(count[:, 1 - s, :], count[:, s, :], both[:, :], ALU.add) \
                        .then_inc(count_rdy, 1)

                def positions(i, s):
                    dve.wait_ge(rank_done, i + 1)
                    nc.vector.tensor_tensor(place[:, :], rank_ps, region[:, :], ALU.add).then_inc(place_rdy, 1)
                    dve.wait_ge(place_rdy, i + 1)
                    for c in range(TOPK):
                        nc.vector.scalar_tensor_tensor(junk[:, c, :], hot[:, c, :], 1.0, place[:, :], ALU.mult,
                                                       ALU.mult, accum_out=posf[:, c:c + 1]).then_inc(posf_rdy, 1)
                    dve.wait_ge(posf_rdy, 2 * i + 2)
                    dve.wait_ge(slo_rdy, 2 * i + 2)
                    dve.wait_ge(tok_rdy, i + 1)
                    nc.vector.tensor_tensor(pos[:, s, :], posf[:, :],
                                            dump[:, bass.ds(i, 1), :].rearrange("p a c -> p (a c)"),
                                            ALU.add).then_inc(pos_rdy, 1)

                dve.wait_ge(const_set, 3)
                dve.wait_ge(const_ld, 64)
                pairs(dve, body)
                choose(NT - 2, 0)
                residual(NT - 1, 1, PAIRS - 1)
                normalise(NT - 1, 1, PAIRS - 1)
                positions(NT - 2, 0)
                choose(NT - 1, 1)
                positions(NT - 1, 1)
                slot_tables(dve)

            @block.tensor
            def _(pe):
                def turn_adj(i, s, g, r):
                    b0, nb = GROUPS[g]
                    n = NG * i + g
                    if g == 0:
                        pe.wait_ge(adj_ld[s], 16 * r + 16 * two(i))
                    need(pe, adj_lo, n - 1)
                    for b in range(nb):
                        last = nc.tensor.transpose(tp[g % 2][:, b * P:(b + 1) * P],
                                                   adj_in[:, s, (b0 + b) * P:(b0 + b + 1) * P], ident[:, :])
                    last.then_inc(tposed, 1)

                def product(i, s, g):
                    b0, nb = GROUPS[g]
                    pe.wait_ge(adj_lo, NG * i + g + 1)
                    if isinstance(i, int) and i == 0:
                        pe.wait_ge(hid_lo, (b0 + nb + 1) // 2)
                    if g == 0:
                        need(pe, x1b, i - 1)
                    for b in range(nb):
                        blk = b0 + b
                        nc.tensor.matmul(acc[s][:, :, :], adjT[:, g % NBUF, 0, b * P:(b + 1) * P],
                                         hid[:, blk, :, :], start=(blk == 0), stop=False, skip_group_check=True)
                        last = nc.tensor.matmul(acc[s][:, 1, :], adjT[:, g % NBUF, 1, b * P:(b + 1) * P],
                                                hid[:, blk, 0, :], start=False, stop=(blk == NT - 1),
                                                skip_group_check=True)
                    last.then_inc(mm_done, 1)

                def turn_norm(i, s):
                    pe.wait_ge(norm2, i + 1)
                    need(pe, nT_rdy, i)
                    for k in range(KD):
                        last = nc.tensor.transpose(small[:, k * P:(k + 1) * P], row[:, s, k * P:(k + 1) * P],
                                                   ident[:, :])
                    last.then_inc(nT_done, 1)

                def gate(i):
                    pe.wait_ge(nT_rdy, i + 1)
                    need(pe, sc_rdy, i)
                    need(pe, place_rdy, i)
                    for k in range(KD):
                        last = nc.tensor.matmul(scores_ps, x1T[:, k, :], wgs[:, k, :], start=(k == 0),
                                                stop=(k == KD - 1))
                    last.then_inc(gate_done, 1)

                def rank(i, s):
                    pe.wait_ge(both_rdy, i + 1)
                    need(pe, count_rdy, i)
                    need(pe, place_rdy, i)
                    nc.tensor.matmul(rank_ps, before[:, :], both[:, :], start=True, stop=False)
                    nc.tensor.matmul(rank_ps, ones[:, :], count[:, s, :], start=False, stop=True) \
                        .then_inc(rank_done, 1)

                def body(r, weights):
                    for s in range(2):
                        i = 2 * r + s
                        first = isinstance(i, int) and i == 0
                        final = isinstance(i, int) and i == NT - 1
                        for g in range(NG):
                            if g + AHEAD < NG:
                                turn_adj(i, s, g + AHEAD, r)
                            elif not final:
                                turn_adj(i + 1, 1 - s, g + AHEAD - NG, r + s)
                            if not first:
                                if g == 4:
                                    turn_norm(i - 1, 1 - s)
                                if g == 5:
                                    gate(i - 1)
                            if g == 3 and not (isinstance(i, int) and i < 2):
                                rank(i - 2, s)
                            product(i, s, g)

                pe.wait_ge(const_set, 3)
                pe.wait_ge(const_ld, 64)
                for g in range(AHEAD):
                    turn_adj(0, 0, g, 0)
                body(0, False)
                with pe.Fori(1, PAIRS - 1) as r:
                    body(r, False)
                body(PAIRS - 1, False)
                rank(NT - 2, 0)
                turn_norm(NT - 1, 1)
                gate(NT - 1)
                rank(NT - 1, 1)
                pe.wait_ge(place_rdy, NT)
                nc.tensor.matmul(total_ps, ones[:, :], count[:, NT % 2, :], start=True, stop=True) \
                    .then_inc(total_done, 1)



        with nc.Block() as block:

            @block.sync
            def _(sp):
                def load_b2(t, s):
                    need(sp, yb_rdy, NH * (t - 1))
                    hold(sp)
                    e = sp.value_load(e_i[0:1, bass.ds(t, 1)], min_val=0, max_val=E - 1)
                    sp.dma_start(b2t[:, s, :], b2[bass.ds(e, 1), :].to_broadcast((P, D))).then_inc(b2_ld[s], 16)

                def body(t, s, q):
                    need(sp, xT_done, t - 1)
                    need(sp, meta_rdy, t - 1)
                    r0 = sp.value_load(base_i[0:1, bass.ds(t, 1)], min_val=0, max_val=XROWS - TOPK - S)
                    sp.dma_start(xr[:, s, :, :], x_rows[bass.ds(r0, S), :].rearrange("(h p) w -> p h w", p=P)) \
                        .then_inc(xr_ld[s], 16)
                    if there(t - 1):
                        load_b2(t - 1, 1 - s)

                tiles(sp, body)
                load_b2(TILES - 1, (TILES - 1) % 2)
                sp.wait_ge(z_st, 16 * NH * TILES)
                sp.dma_start(out[0:N16, :], sums[0:N16, :]).then_inc(out_st, 16)
                sp.dma_start(out[N16:N, :], sums[N16:N, :]).then_inc(out_st, 16)
                sp.wait_ge(out_st, 32)

            @block.scalar
            def _(act):
                act.wait_ge(b1_done, 1)
                nc.scalar.activation(b1t[:, :], b1_ps, ACT.Copy, scale=S_H).then_inc(b1_rdy, 1)

                def x_hi(t, s):
                    act.wait_ge(xT_done, t + 1)
                    need(act, h_done, KB * (t - 1))
                    nc.scalar.activation(xT[:, s, 0, :, :], xT_ps, ACT.Copy, scale=S_X).then_inc(xT_hi, 1)

                def hidden_hi(t, s):
                    for a in range(KB):
                        act.wait_ge(h32_rdy, KB * t + a + 1)
                        need(act, y_done, NH * (t - 1))
                        nc.scalar.activation(hsp[:, s, 0, 2 * a:2 * a + 2, :], h32[:, a % 2, :, :], ACT.Relu) \
                            .then_inc(h_hi, 1)

                def copy_meta(t, s):
                    need(act, zi_rdy, t - 1)
                    need(act, high_rdy, t - 1)
                    nc.scalar.activation(meta[:, s, :, :], xr[:, s, :, D:XW], ACT.Copy).then_inc(meta_rdy, 1)

                def exps(t, s):
                    need(act, ssum_rdy, t - 1)
                    need(act, wn_rdy, t - 1)
                    act.wait_ge(meta_rdy, t + 1)
                    nc.scalar.activation(sexp[:, s, :, :], meta[:, s, :, 0:TOPK], ACT.Exp).then_inc(sexp_rdy, 1)

                def weigh(t, s):
                    for h in range(NH):
                        act.wait_ge(yb_rdy, NH * t + h + 1)
                        act.wait_ge(wt_rdy, t + 1)
                        need(act, z_st, 16 * (NH * (t - 2) + h + 1))
                        nc.scalar.activation(yrow[:, s, h, :], ysum[:, h, :], ACT.Copy, scale=wt[:, s, h:h + 1]) \
                            .then_inc(y_rdy, 1)

                def body(t, s, q):
                    if there(t - 1):
                        weigh(t - 1, 1 - s)
                    if there(t + 2):
                        x_hi(t + 2, s)
                        copy_meta(t + 2, s)
                    if there(t + 1):
                        exps(t + 1, 1 - s)
                        hidden_hi(t + 1, 1 - s)

                for t in range(2):
                    x_hi(t, t)
                    copy_meta(t, t)
                exps(0, 0)
                hidden_hi(0, 0)
                tiles(act, body)
                weigh(TILES - 1, (TILES - 1) % 2)

            @block.gpsimd
            def _(pool):
                def gate_weights(t, s):
                    pool.wait_ge(meta_rdy, t + 1)
                    need(pool, z_st, 16 * NH * (t - 1))
                    hold(pool)
                    nc.gpsimd.tensor_copy(zi[:, s, :], meta[:, s, :, C_TOK - D]).then_inc(zi_rdy, 1)
                    pool.wait_ge(sexp_rdy, t + 1)
                    nc.gpsimd.tensor_tensor(wd[:, s, :], sexp[:, s, :, 1], sexp[:, s, :, 0], ALU.subtract) \
                        .then_inc(wd_rdy, 1)
                    nc.gpsimd.tensor_tensor(ssum[:, s, :], sexp[:, s, :, 1], sexp[:, s, :, 0], ALU.add) \
                        .then_inc(ssum_rdy, 1)
                    pool.wait_ge(wd_rdy, t + 1)
                    pool.wait_ge(high_rdy, t + 1)
                    nc.gpsimd.tensor_tensor(wf[:, s, :], wd[:, s, :], high[:, s, :], ALU.mult).then_inc(wf_rdy, 1)
                    pool.wait_ge(wf_rdy, t + 1)
                    need(pool, wt_rdy, t - 1)
                    nc.gpsimd.tensor_tensor(wn[:, s, :], wf[:, s, :], sexp[:, s, :, 0], ALU.add).then_inc(wn_rdy, 1)

                def scatter(t, s):
                    for h in range(NH):
                        pool.wait_ge(y_rdy, NH * t + h + 1)
                        need(pool, z_st, 16 * (NH * t + h))
                        hold(pool)
                        nc.gpsimd.indirect_dma_start(
                            out=sums, out_offset=bass.IndirectOffsetOnAxis(ap=zi[:, s, h:h + 1].bitcast(u32), axis=0),
                            in_=yrow[:, s, h, :], in_offset=None, compute_op=ALU.add).then_inc(z_st, 16)

                def body(t, s, q):
                    if there(t - 1):
                        scatter(t - 1, 1 - s)
                    if there(t + 1):
                        gate_weights(t + 1, 1 - s)

                gate_weights(0, 0)
                tiles(pool, body)
                scatter(TILES - 1, (TILES - 1) % 2)

            @block.vector
            def _(dve):
                def x_lo(t, s):
                    dve.wait_ge(xT_hi, t + 1)
                    nc.vector.scalar_tensor_tensor(xT[:, s, 1, :, :], xT_ps, S_X, xT[:, s, 0, :, :], ALU.mult,
                                                   ALU.subtract).then_inc(xT_lo, 1)

                def which(t, s):
                    dve.wait_ge(meta_rdy, t + 1)
                    need(dve, wf_rdy, t - 1)
                    nc.vector.tensor_scalar(high[:, s, :], meta[:, s, :, C_ELO - D], e_f[:, bass.ds(t, 1)], None,
                                            ALU.is_lt).then_inc(high_rdy, 1)

                def hidden(t, s):
                    e = dve.value_load(e_i[0:1, bass.ds(t, 1)], min_val=0, max_val=E - 1)

                    def bias(a):
                        dve.wait_ge(h_done, KB * t + a + 1)
                        need(dve, h_lo, KB * t + a - 1)
                        nc.vector.scalar_tensor_tensor(
                            h32[:, a % 2, :, :], h_ps[a], S_H / (S_X * S_W),
                            b1t[:, bass.ds(e * KH + 2 * a, 2)].rearrange("p (c z) -> p c z", z=1)
                            .to_broadcast((P, 2, S)), ALU.mult, ALU.add).then_inc(h32_rdy, 1)

                    def low(a):
                        dve.wait_ge(h_hi, KB * t + a + 1)
                        nc.vector.scalar_tensor_tensor(
                            hsp[:, s, 1, 2 * a:2 * a + 2, :], h32[:, a % 2, :, :], 0.0,
                            hsp[:, s, 0, 2 * a:2 * a + 2, :], ALU.max, ALU.subtract).then_inc(h_lo, 1)

                    for a in range(KB):
                        bias(a)
                        if a:
                            low(a - 1)
                    low(KB - 1)

                def weights(t, s):
                    dve.wait_ge(ssum_rdy, t + 1)
                    nc.vector.reciprocal(srec[:, s, :], ssum[:, s, :]).then_inc(srec_rdy, 1)
                    dve.wait_ge(srec_rdy, t + 1)
                    dve.wait_ge(wn_rdy, t + 1)
                    need(dve, y_rdy, NH * (t - 1))
                    nc.vector.tensor_tensor(wt[:, s, :], wn[:, s, :], srec[:, s, :], ALU.mult).then_inc(wt_rdy, 1)

                def result(t, s, q):
                    dve.wait_ge(b2_ld[s], 16 * (q + 1))
                    for h in range(NH):
                        dve.wait_ge(y_done, NH * t + h + 1)
                        need(dve, y_rdy, NH * (t - 1) + h + 1)
                        nc.vector.scalar_tensor_tensor(ysum[:, h, :], acc[h][:, 0, :], 1.0 / (S_H * S_W),
                                                       b2t[:, s, :], ALU.mult, ALU.add).then_inc(ya_rdy, 1)
                        dve.wait_ge(ya_rdy, NH * t + h + 1)
                        nc.vector.scalar_tensor_tensor(ysum[:, h, :], acc[h][:, 1, :], 1.0 / (S_H * S_W),
                                                       ysum[:, h, :], ALU.mult, ALU.add).then_inc(yb_rdy, 1)

                def body(t, s, q):
                    if there(t - 1):
                        result(t - 1, 1 - s, q + s - 1)
                        weights(t - 1, 1 - s)
                    if there(t + 2):
                        x_lo(t + 2, s)
                    if there(t + 1):
                        hidden(t + 1, 1 - s)
                        which(t + 1, 1 - s)

                x_lo(0, 0)
                x_lo(1, 1)
                dve.wait_ge(b1_rdy, 1)
                hidden(0, 0)
                which(0, 0)
                tiles(dve, body)
                last = TILES - 1
                result(last, last % 2, last // 2)
                weights(last, last % 2)

            @block.tensor
            def _(pe):
                nc.tensor.transpose(b1_ps, b1r[:, :], ident[0:E * KH, 0:E * KH]).then_inc(b1_done, 1)

                def turn(t, s, q):
                    pe.wait_ge(xr_ld[s], 16 * (q + 1))
                    need(pe, xT_lo, t)
                    for k in range(KD):
                        for h in range(NH):
                            last = nc.tensor.transpose(xT_ps[:, k, h * P:(h + 1) * P],
                                                       xr[:, s, h, k * P:(k + 1) * P], ident[:, :])
                    last.then_inc(xT_done, 1)

                def up(t, s):
                    e = pe.value_load(e_i[0:1, bass.ds(t, 1)], min_val=0, max_val=E - 1)
                    pe.wait_ge(xT_lo, t + 1)
                    for c in range(KH):
                        if c % 2 == 0:
                            need(pe, h32_rdy, KB * (t - 1) + c // 2 + 1)
                        for k in range(KD):
                            for n, (wv, xv) in enumerate(((0, 0), (0, 1), (1, 0))):
                                w = w1s[:, bass.ds(e, 1), wv, k, c * P:(c + 1) * P].rearrange("p a n -> p (a n)")
                                last = nc.tensor.matmul(h_ps[c // 2][:, c % 2, :], w, xT[:, s, xv, k, :],
                                                        start=(k == 0 and n == 0), stop=(k == KD - 1 and n == 2))
                        if c % 2:
                            last.then_inc(h_done, 1)

                def down(t, s):
                    e = pe.value_load(e_i[0:1, bass.ds(t, 1)], min_val=0, max_val=E - 1)
                    for c in range(KH):
                        if c % 2 == 0:
                            pe.wait_ge(h_lo, KB * t + c // 2 + 1)
                        w = w2s[:, bass.ds(e, 1), c, :, :].rearrange("p a v d -> p (a v) d")
                        for h in range(NH):
                            if c == 0:
                                need(pe, yb_rdy, NH * (t - 1) + h + 1)
                            at = slice(h * P, (h + 1) * P)
                            nc.tensor.matmul(acc[h][:, :, :], hsp[:, s, 0, c, at], w, start=(c == 0), stop=False,
                                             skip_group_check=True)
                            last = nc.tensor.matmul(acc[h][:, 1, :], hsp[:, s, 1, c, at], w[:, 0, :], start=False,
                                                    stop=(c == KH - 1), skip_group_check=True)
                            if c == KH - 1:
                                last.then_inc(y_done, 1)

                def body(t, s, q):
                    if there(t + 2):
                        turn(t + 2, s, q + 1)
                    if there(t + 1):
                        up(t + 1, 1 - s)
                    down(t, s)

                turn(0, 0, 0)
                turn(1, 1, 0)
                pe.wait_ge(b1_rdy, 1)
                up(0, 0)
                tiles(pe, body)


_INS = ["x", "adj", "L0_gnn_W", "L0_ffn_W1", "L0_ffn_b1", "L0_ffn_W2", "L0_ffn_b2", "L0_ffn_Wg", "L0_ffn_bg"]
_OUTS = [((N, D), "float32")]


def kernel(**inputs):
    import numpy as _np
    import concourse.bacc as _bacc
    from concourse import mybir as _mybir
    from concourse.bass_utils import run_bass_kernel_spmd as _run

    nc = _bacc.Bacc("TRN2", target_bir_lowering=False, num_devices=1)
    arrays, args = {}, []
    for name in _INS:
        a = _np.ascontiguousarray(inputs[name])
        arrays[f"in_{name}_dram"] = a
        args.append(nc.dram_tensor(f"in_{name}_dram", a.shape, _mybir.dt.from_np(a.dtype), kind="ExternalInput").ap())
    for i, (shape, dtype) in enumerate(_OUTS):
        dt = _mybir.dt.from_np(_np.dtype(dtype))
        args.append(nc.dram_tensor(f"out_{i}_dram", shape, dt, kind="ExternalOutput").ap())
    gnn_moe(nc, *args)
    r = _run(nc, [arrays], core_ids=[0])
    return r.results[0]["out_0_dram"]
```

```python
import concourse.bass as bass
from concourse import mybir
from contextlib import ExitStack, contextmanager


f32 = mybir.dt.float32
f16 = mybir.dt.float16
bf16 = mybir.dt.bfloat16
i32 = mybir.dt.int32
u32 = mybir.dt.uint32
ALU = mybir.AluOpType
ACT = mybir.ActivationFunctionType
AX = mybir.AxisListType

P = 128
N = 3327
D = 256
H = 1024
E = 8
TOPK = 2
EPS = 1e-5
NT = (N + P - 1) // P
NP = NT * P
LAST = N - (NT - 1) * P
LAST16 = LAST // 16 * 16
KD = D // P
KH = H // P

GROUPS = [(0, 5), (5, 5), (10, 4), (14, 4), (18, 4), (22, 4)]
NG = len(GROUPS)
GW = 5 * P
NBUF = 3
AHEAD = 2
PAIRS = NT // 2
FIRST = AHEAD * GW

S_ADJ = 2.0 ** 6
S_HID = 2.0 ** 4
S_W = 2.0 ** 8
S_X = 2.0 ** 5
S_H = 2.0 ** 4

NH = 2
S = NH * P
TILES = (TOPK * N + E * (S - 1)) // S
LEAST = (TOPK * N + S - 1) // S
CAP = (N + S - 1) // S * S + S
SPARE = E * CAP
DUMP = SPARE + (TILES - LEAST) * S
XROWS = DUMP + TOPK
C_SLO, C_SHI, C_ELO, C_TOK, XW = D, D + 1, D + 2, D + 3, D + 4
OROWS = NP + S


def gnn_moe(nc, x, adj, gnn_w, w1, b1, w2, b2, wg, bg, out):
    ctx = ExitStack()
    with ctx:
        def sb(name, shape, dt):
            return ctx.enter_context(nc.sbuf_tensor(name, shape, dt))

        def pb(name, shape, dt=f32):
            return ctx.enter_context(nc.psum_tensor(name, shape, dt))

        def sem(name):
            return ctx.enter_context(nc.semaphore(name))

        x_rows = nc.dram_tensor("x_rows", [XROWS, XW], f32, kind="Internal").ap()

        w1s = sb("w1s", [P, E, 2, KD, H], f16)
        w2s = sb("w2s", [P, E, KH, 2, D], f16)
        hid = sb("hid", [P, NT, 2, D], f16)
        adj_in = sb("adj_in", [P, 2, NP], f32)
        adjT = sb("adjT", [P, NBUF, 2, GW], f16)
        wst = sb("wst", [P, 2, H], f32)
        xin = sb("xin", [P, 2, D], f32)
        row = sb("row", [P, 2, XW], f32)
        padrow = sb("padrow", [P, NH, XW], f32)
        x1T = sb("x1T", [P, KD, P], f32)
        ident = sb("ident", [P, P], f32)
        before = sb("before", [P, P], bf16)
        ones = sb("ones", [P, P], bf16)
        wrow = sb("wrow", [P, D], f32)
        wgs = sb("wgs", [P, KD, E], f32)
        bgs = sb("bgs", [P, E], f32)
        b1r = sb("b1r", [E * KH, P], f32)
        b1t = sb("b1t", [P, E * KH], f32)
        stats = sb("stats", [P, 6], f32)
        mv = sb("mv", [P, 2], f32)
        sd = sb("sd", [P, 1], f32)
        rstd = sb("rstd", [P, 1], f32)
        iota_i = sb("iota_i", [P, TILES], i32)
        iota_e = sb("iota_e", [P, E], f32)
        iota_t = sb("iota_t", [P, TILES], f32)
        region = sb("region", [P, E], f32)
        tok_i = sb("tok_i", [P, NT], i32)
        tok = sb("tok", [P, NT], f32)
        live = sb("live", [P, NT], f32)
        dump = sb("dump", [P, NT, TOPK], f32)
        pad_i = sb("pad_i", [P, NH], i32)
        score = sb("score", [P, E], f32)
        top = sb("top", [P, E], f32)
        below = sb("below", [P, E], f32)
        topix = sb("topix", [P, E], u32)
        topf = sb("topf", [P, TOPK], f32)
        ehi = sb("ehi", [P, 1], f32)
        hot = sb("hot", [P, TOPK, E], f32)
        both = sb("both", [P, E], bf16)
        count = sb("count", [P, 2, E], bf16)
        place = sb("place", [P, E], f32)
        junk = sb("junk", [P, TOPK, E], f32)
        posf = sb("posf", [P, TOPK], f32)
        pos = sb("pos", [P, 2, TOPK], i32)
        epsc = sb("epsc", [P, 1], f32)
        epsx = sb("epsx", [P, 1], f32)
        x_all = w2s[:, E // 2:E].rearrange("p e k s d -> p (e k s d)").bitcast(f32)[:, 0:NT * D] \
            .rearrange("p (t d) -> p t d", t=NT)
        stats_x = wst[:, 0, 0:NT * 6].rearrange("p (t n) -> p t n", t=NT)
        mv_x = wst[:, 0, 160:160 + 2 * NT].rearrange("p (t n) -> p t n", t=NT)
        sd_x, rstd_x, shift_x = (wst[:, 0, 224 + 32 * n:224 + 32 * n + NT] for n in range(3))

        tp = [pb(f"tp{i}", [P, 1024]) for i in range(2)]
        acc = [pb(f"acc{i}", [P, 2, D]) for i in range(2)]
        small = pb("small", [P, 512])
        gate_ps = pb("gate_ps", [P, 512])
        scores_ps = gate_ps[:, 0:E]
        rank_ps = gate_ps[:, 128:128 + E]
        total_ps = small[:, 256:256 + E]

        const_set, const_ld = sem("const_set"), sem("const_ld")
        XCUT = [0, 4, 10, 18, NT - 1]
        XPARTS = list(zip(XCUT, [*XCUT[1:-1], NT]))
        x_in = [sem(f"x_in{n}") for n in range(len(XCUT))]
        tail_zero, ident_rdy = sem("tail_zero"), sem("ident_rdy")
        wrow_ld, adj_first = sem("wrow_ld"), sem("adj_first")
        stats1, mv1, sd1, rstd1, shift1, centred, norm1, times_w, even_hi, odd_hi, even_lo, odd_lo = [
            sem(s) for s in ("stats1", "mv1", "sd1", "rstd1", "shift1", "centred", "norm1", "times_w",
                             "even_hi", "odd_hi", "even_lo", "odd_lo")]
        adj_ld = [sem(f"adj_ld{i}") for i in range(2)]
        tposed, adj_hi, adj_lo, mm_done = [sem(s) for s in ("tposed", "adj_hi", "adj_lo", "mm_done")]
        xin_ld = [sem(f"xin_ld{i}") for i in range(2)]
        x1_st = [sem(f"x1_st{i}") for i in range(2)]
        x1a, x1b, st2, mv2, sd2, rstd2, norm2, tok_rdy = [
            sem(s) for s in ("x1a", "x1b", "st2", "mv2", "sd2", "rstd2", "norm2", "tok_rdy")]
        nT_done, nT_rdy, gate_done = sem("nT_done"), sem("nT_rdy"), sem("gate_done")
        sc_rdy, top_rdy, below_rdy, ix_rdy, ixf_rdy, e_rdy, hot_rdy, both_rdy, slo_rdy, count_rdy = [
            sem(s) for s in ("sc_rdy", "top_rdy", "below_rdy", "ix_rdy", "ixf_rdy", "e_rdy", "hot_rdy", "both_rdy", "slo_rdy",
                             "count_rdy")]
        rank_done, place_rdy, posf_rdy, pos_rdy = [
            sem(s) for s in ("rank_done", "place_rdy", "posf_rdy", "pos_rdy")]
        sent = [sem(f"sent{i}") for i in range(2)]
        spare_st = sem("spare_st")
        w_ld = [sem(f"w_ld{i}") for i in range(2)]
        w_sc, w_hi, w_lo = sem("w_sc"), sem("w_hi"), sem("w_lo")

        def need(eng, s, v):
            if not isinstance(v, int) or v > 0:
                eng.wait_ge(s, v)

        def hold(eng):
            eng.nop(nofuse=True)

        HIDDEN_BY = [
            [("stats", 4), ("root", 0), ("pair", 0), ("stats", 6), ("pair", 1), ("stats", 10),
             ("root", 1), ("pair", 2)],
            [("pair", 3), ("pair", 4), ("stats", 14)],
            [("stats", 18), ("root", 2), ("pair", 5), ("pair", 6), ("stats", 20)],
            [("pair", 7), ("stats", 24)],
            [("pair", 8), ("stats", NT), ("root", 3), ("pair", 9), ("pair", 10)],
            [("pair", 11), ("pair", 12), ("pair", 13)]]

        def pairs(eng, body):
            body(0, False)
            body(1, True)
            with eng.Fori(2, E + 1) as r:
                body(r, True)
            with eng.Fori(E + 1, PAIRS - 1) as r:
                body(r, False)
            body(PAIRS - 1, False)

        def load_rows(eng, dst, src, i, s):
            if isinstance(i, int) and i == NT - 1:
                eng.dma_start(dst[0:LAST16], src[i * P:i * P + LAST16, :]).then_inc(s, 16)
                eng.dma_start(dst[LAST16:LAST], src[i * P + LAST16:N, :]).then_inc(s, 16)
            else:
                eng.dma_start(dst, src[bass.ds(i * P, P), :]).then_inc(s, 16)

        def part_of(t):
            return [t < t1 for _, t1 in XPARTS].index(True)

        def pad(eng, experts):
            for e in experts:
                r0 = eng.value_load(padat[0:1, e:e + 1], min_val=0, max_val=SPARE - S)
                eng.dma_start(x_rows[bass.ds(r0, S), :].rearrange("(h p) w -> p h w", p=P), padrow[:, :, :]) \
                    .then_inc(pad_st, 16)

        def two(i):
            return 2 if isinstance(i, int) and i == NT - 1 else 1

        def words(region):
            return region.rearrange("p a b c -> p (a b c)").bitcast(f32)

        KB = KH // 2
        pool_f = words(hid[:, :, :, :])
        hsp = pool_f[:, 0:4096].bitcast(f16).rearrange("p (s v c n) -> p s v c n", s=2, v=2, c=KH)
        ysum = pool_f[:, 5120:5120 + NH * D].rearrange("p (h d) -> p h d", h=NH)
        b2t = pool_f[:, 5632:5632 + 2 * D].rearrange("p (s d) -> p s d", s=2)
        pool_t = adj_in[:, :, :].rearrange("p a b -> p (a b)")
        yrow = pool_t[:, 0:2 * NH * D].rearrange("p (s h d) -> p s h d", s=2, h=NH)
        xr = pool_t[:, 1024:1024 + 2 * NH * XW].rearrange("p (s h w) -> p s h w", s=2, h=NH)
        h32 = pool_t[:, 3584:3584 + KB * 2 * S].rearrange("p (a c n) -> p a c n", a=KB, c=2)
        xT = pool_t[:, 2560:3584].bitcast(f16).rearrange("p (s v k n) -> p s v k n", s=2, v=2, k=KD)
        pool_w = wst[:, :, :].rearrange("p a b -> p (a b)")
        cmp_n = pool_w[:, 0:E * NT].rearrange("p (e k) -> p e k", e=E)
        cmp_t = pool_w[:, 512:512 + TILES * E].rearrange("p (t e) -> p t e", e=E)
        cmp_w = pool_w[:, 1024:1024 + TILES * E].rearrange("p (t e) -> p t e", e=E)
        e_raw, start_t, base_f = (pool_w[:, 1536 + 64 * i:1536 + 64 * i + TILES] for i in range(3))
        h_ps = [tp[a // 2][:, 512 * (a % 2):512 * (a % 2) + 512].rearrange("p (c n) -> p c n", c=2)
                for a in range(KB)]
        xT_ps = small[:, :].rearrange("p (k n) -> p k n", k=KD)
        b1_ps = acc[0][:, 0, 0:E * KH]

        KT = -(-N // S)
        thr = sb("thr", [P, KT], f32)
        one_e = sb("one_e", [P, E], f32)
        filled = sb("filled", [P, E], f32)
        cum = sb("cum", [P, E], f32)
        e_f = sb("e_f", [P, TILES], f32)
        e_i = sb("e_i", [P, TILES], i32)
        base_i = sb("base_i", [P, TILES], i32)
        used_i = pool_w[:, 1920:1921].bitcast(i32)
        code = pool_w[:, 1984:1985 + TILES].bitcast(i32)
        start_e, end_e = pool_w[:, 256:256 + E], pool_w[:, 288:288 + E]
        half_at, ends = (pool_w[:, 896 + 64 * i:896 + 64 * i + TILES] for i in range(2))
        padat = sb("padat", [P, E], i32)
        sexp = pool_w[:, 1792:1800].rearrange("p (s h c) -> p s h c", s=2, h=NH)
        ssum, srec, high, wd, wf, wn, wt = (
            pool_w[:, 1800 + 4 * n:1804 + 4 * n].rearrange("p (s h) -> p s h", s=2) for n in range(7))
        meta = pool_w[:, 1840:1840 + 2 * NH * (XW - D)].rearrange("p (s h w) -> p s h w", s=2, h=NH)
        zi = sb("zi", [P, 2, NH], i32)

        total_done, tstep, pads_known, b1_done, b1_rdy, pad_st = [
            sem(s) for s in ("total_done", "tstep", "pads_known", "b1_done", "b1_rdy", "pad_st")]
        xr_ld = [sem(f"xr_ld{i}") for i in range(2)]
        b2_ld = [sem(f"b2_ld{i}") for i in range(2)]
        xT_done, xT_hi, xT_lo, h_done, h32_rdy, h_hi, h_lo, y_done, ya_rdy, yb_rdy, y_rdy, z_st = [
            sem(s) for s in ("xT_done", "xT_hi", "xT_lo", "h_done", "h32_rdy", "h_hi", "h_lo", "y_done", "ya_rdy",
                             "yb_rdy", "y_rdy", "z_st")]
        meta_rdy = sem("meta_rdy")
        sexp_rdy, ssum_rdy, srec_rdy, high_rdy, zi_rdy, wd_rdy, wf_rdy, wn_rdy, wt_rdy = [
            sem(s) for s in ("sexp_rdy", "ssum_rdy", "srec_rdy", "high_rdy", "zi_rdy", "wd_rdy", "wf_rdy",
                             "wn_rdy", "wt_rdy")]
        BUSY = 26
        SURE = (LEAST - 2) // 2

        def tiles(eng, body):
            @contextmanager
            def sure(t):
                yield t

            @contextmanager
            def if_used(t):
                with eng.If(used > t):
                    yield t.with_bounds(min_val=0, max_val=TILES - 1)

            for t in range(4):
                body(t, t % 2, t // 2, sure)
            used = eng.value_load(used_i[0:1, 0:1], min_val=LEAST, max_val=TILES)
            with eng.Fori(2, SURE) as q:
                for s in range(2):
                    body(2 * q + s, s, q, sure)
            with eng.Fori(SURE, TILES // 2 + 1) as q:
                for s in range(2):
                    body(2 * q + s, s, q, if_used)

        def there(t):
            return not isinstance(t, int) or t >= 0

        with nc.Block() as block:

            @block.sync
            def _(sp):
                def load_x(n):
                    t0, t1 = XCUT[n], XCUT[n + 1]
                    sp.dma_start(x_all[:, t0:t1, :],
                                 x[t0 * P:t1 * P, :].rearrange("(t p) d -> p t d", p=P)).then_inc(x_in[n], 16)

                load_x(0)
                load_x(1)
                sp.dma_start(adj_in[:, 0, 0:FIRST], adj[0:P, 0:FIRST]).then_inc(adj_first, 16)
                load_x(2)
                sp.dma_start(adj_in[:, 0, FIRST:N], adj[0:P, FIRST:N]).then_inc(adj_ld[0], 16)
                load_x(3)
                sp.wait_ge(tail_zero, 1)
                load_rows(sp, x_all[:, NT - 1, :], x, NT - 1, x_in[-1])
                sp.dma_start(wgs[:, :, :], wg.rearrange("(k p) e -> p k e", p=P)).then_inc(const_ld, 16)
                sp.dma_start(bgs[:, :], bg.rearrange("(a e) -> a e", a=1).to_broadcast((P, E))) \
                    .then_inc(const_ld, 16)
                sp.dma_start(b1r[:, :], b1.rearrange("e (c p) -> (e c) p", p=P)).then_inc(const_ld, 16)

                def load_weights(e, u):
                    src = w1[bass.ds(e, 1), u * P:(u + 1) * P, :].rearrange("a p h -> p (a h)") if u < KD else \
                        w2[bass.ds(e, 1), (u - KD) * 4 * P:(u - KD + 1) * 4 * P, :] \
                        .rearrange("a (c p) d -> p (a c) d", p=P)
                    dst = wst[:, u % 2, :] if u < KD else wst[:, u % 2, :].rearrange("p (c d) -> p c d", c=4)
                    sp.dma_start(dst, src).then_inc(w_ld[u % 2], 16)

                def body(r, weights):
                    for s in range(2):
                        i = 2 * r + s
                        need(sp, tposed, NG * (i - 1))
                        if not (isinstance(i, int) and i == 0):
                            load_rows(sp, adj_in[:, s, 0:N], adj, i, adj_ld[s])
                        if not (isinstance(i, int) and i < 2):
                            store_x1(i - 2, s)
                            sp.wait_ge(x1_st[s], 16 * r)
                            sp.wait_ge(norm2, i - 1)
                        load_rows(sp, xin[:, s, :], x, i, xin_ld[s])
                        if weights:
                            for u in (2 * s, 2 * s + 1):
                                sp.wait_ge(w_lo, 4 * r + u - 2 - 1)
                                load_weights(r - 1, u)

                def store_x1(i, s):
                    sp.wait_ge(x1b, i + 1)
                    sp.dma_start(out[bass.ds(i * P, P), :], xin[:, s, :]).then_inc(x1_st[s], 16)

                pairs(sp, body)
                for s in range(2):
                    store_x1(NT - 2 + s, s)
                sp.wait_ge(pads_known, 1)
                pad(sp, range(0, E // 2))
                for s in range(2):
                    sp.wait_ge(x1_st[s], 16 * PAIRS)

            @block.scalar
            def _(act):
                act.dma_start(wrow[:, :], gnn_w.rearrange("(a d) -> a d", a=1).to_broadcast((P, D))) \
                    .then_inc(wrow_ld, 16)
                act.wait_ge(const_set, 1)
                nc.scalar.activation(sd[:, :], epsx[:, :], ACT.Sqrt)

                def roots(q):
                    t0, t1 = XPARTS[q]
                    act.wait_ge(mv1, t1)
                    nc.scalar.activation(sd_x[:, t0:t1], mv_x[:, t0:t1, 1], ACT.Sqrt, bias=epsx[:, :],
                                         scale=1.0 / S_HID ** 2).then_inc(sd1, 1)

                def hidden_pair(j):
                    if j < PAIRS:
                        t = 2 * j + 1
                        act.wait_ge(shift1, part_of(t) + 1)
                        nc.scalar.activation(x_all[:, t, :], x_all[:, t, :], ACT.Identity,
                                             bias=shift_x[:, t:t + 1], scale=rstd_x[:, t:t + 1]).then_inc(norm1, 1)
                        act.wait_ge(centred, j + 1)
                        nc.scalar.activation(hid[:, 2 * j, 0, :], x_all[:, 2 * j, :], ACT.Copy,
                                             scale=rstd_x[:, 2 * j:2 * j + 1]).then_inc(even_hi, 1)
                    if j:
                        act.wait_ge(times_w, j)
                        nc.scalar.activation(hid[:, 2 * j - 1, 0, :], x_all[:, 2 * j - 1, :],
                                             ACT.Copy).then_inc(odd_hi, 1)

                def body(r, weights):
                    for s in range(2):
                        i = 2 * r + s
                        for g, (b0, nb) in enumerate(GROUPS):
                            n = NG * i + g
                            if isinstance(i, int) and i == 0:
                                for what, n0 in HIDDEN_BY[g]:
                                    if what == "root":
                                        roots(n0)
                                    elif what == "pair":
                                        hidden_pair(n0)
                            act.wait_ge(tposed, n + 1)
                            need(act, mm_done, n - NBUF + 1)
                            nc.scalar.activation(adjT[:, g % NBUF, 0, 0:nb * P], tp[g % 2][:, 0:nb * P],
                                                 ACT.Copy, scale=S_ADJ).then_inc(adj_hi, 1)
                            if g == 3 and not (isinstance(i, int) and i == 0):
                                root(i - 1, 1 - s)
                            if g == 5 and not (isinstance(i, int) and i == 0):
                                gate_in(i - 1)
                            if weights and g in (1, 4):
                                split(r - 1, 2 * s + (g == 4))

                def root(i, s):
                    act.wait_ge(mv2, i + 1)
                    nc.scalar.activation(sd[:, :], mv[:, 1:2], ACT.Sqrt, bias=epsc[:, :]).then_inc(sd2, 1)

                def gate_in(i):
                    act.wait_ge(nT_done, i + 1)
                    need(act, gate_done, i)
                    nc.scalar.activation(x1T[:, :, :], small[:, 0:D].rearrange("p (k n) -> p k n", k=KD),
                                         ACT.Copy).then_inc(nT_rdy, 1)

                def split(e, u):
                    unit = 4 * e + u
                    act.wait_ge(w_ld[u % 2], 32 * e + 16 * (u // 2) + 16)
                    nc.scalar.activation(wst[:, u % 2, :], wst[:, u % 2, :], ACT.Copy, scale=S_W).then_inc(w_sc, 1)
                    act.wait_ge(w_sc, unit + 1)
                    dst = w1s[:, bass.ds(e, 1), 0, u, :].rearrange("p a h -> p (a h)") if u < KD else \
                        w2s[:, bass.ds(e, 1), (u - KD) * 4:(u - KD) * 4 + 4, 0, :].rearrange("p a c d -> p (a c) d")
                    src = wst[:, u % 2, :] if u < KD else wst[:, u % 2, :].rearrange("p (c d) -> p c d", c=4)
                    nc.scalar.activation(dst, src, ACT.Copy).then_inc(w_hi, 1)

                pairs(act, body)
                root(NT - 1, 1)
                gate_in(NT - 1)
                act.wait_ge(pads_known, 1)
                pad(act, range(E // 2, E))

            @block.gpsimd
            def _(pool):
                nc.gpsimd.memset(x_all[96:P, NT - 1, :], 0.0).then_inc(tail_zero, 1)
                pool.wait_ge(tail_zero, 1)
                nc.gpsimd.memset(epsx[:, :], EPS / S_HID ** 2).then_inc(const_set, 1)
                nc.gpsimd.memset(adj_in[:, :, N:NP], 0.0)
                nc.gpsimd.memset(ident[:, :], 0.0).then_inc(ident_rdy, 1)
                pool.wait_ge(ident_rdy, 1)
                nc.gpsimd.affine_select(out=ident[:, :], in_=ident[:, :], compare_op=ALU.not_equal, fill=1.0,
                                        base=0, pattern=[[-1, P]], channel_multiplier=1).then_inc(ident_rdy, 1)
                nc.gpsimd.memset(epsc[:, :], EPS)
                nc.gpsimd.memset(before[:, :], 0.0)
                nc.gpsimd.memset(ones[:, :], 1.0)
                nc.gpsimd.memset(live[:, :], 1.0)
                nc.gpsimd.memset(dump[:, :, :], 0.0)
                nc.gpsimd.memset(padrow[:, :, :], 0.0)
                nc.gpsimd.memset(count[:, 0, :], 0.0)
                nc.gpsimd.iota(iota_i[:, :], [[1, TILES]], base=0, channel_multiplier=0)
                nc.gpsimd.iota(tok_i[:, :], [[P, NT]], base=0, channel_multiplier=1)
                nc.gpsimd.iota(pad_i[:, :], [[P, NH]], base=NP, channel_multiplier=1).then_inc(const_set, 1)
                pool.wait_ge(wrow_ld, 16)
                for j in range(PAIRS + 1):
                    if j < PAIRS:
                        t = 2 * j + 1
                        pool.wait_ge(norm1, j + 1)
                        nc.gpsimd.tensor_tensor(x_all[:, t, :], x_all[:, t, :], wrow[:, :], ALU.mult) \
                            .then_inc(times_w, 1)
                    if j:
                        t = 2 * j - 1
                        pool.wait_ge(odd_hi, j)
                        nc.gpsimd.tensor_tensor(hid[:, t, 1, :], x_all[:, t, :], hid[:, t, 0, :],
                                                ALU.subtract).then_inc(odd_lo, 1)
                pool.wait_ge(const_set, 2)
                nc.gpsimd.affine_select(out=before[:, :], in_=before[:, :], compare_op=ALU.is_ge, fill=1.0,
                                        base=0, pattern=[[-1, P]], channel_multiplier=1)
                end = (NT - 1) * P + LAST
                nc.gpsimd.affine_select(out=live[:, :], in_=live[:, :], compare_op=ALU.not_equal, fill=0.0,
                                        base=-end, pattern=[[P, NT]], channel_multiplier=1)
                for c in range(TOPK):
                    nc.gpsimd.affine_select(out=dump[:, :, c], in_=dump[:, :, c], compare_op=ALU.not_equal,
                                            fill=float(DUMP + c), base=-end, pattern=[[P, NT]],
                                            channel_multiplier=1)
                nc.gpsimd.tensor_copy(iota_e[:, :], iota_i[:, 0:E])
                nc.gpsimd.tensor_copy(iota_t[:, :], iota_i[:, :])
                nc.gpsimd.tensor_copy(tok[:, :], tok_i[:, :])
                nc.gpsimd.tensor_scalar(region[:, :], iota_i[:, 0:E], float(CAP), None, ALU.mult)
                nc.gpsimd.tensor_copy(padrow[:, :, C_TOK], pad_i[:, :]).then_inc(const_set, 1)
                pool.wait_ge(const_set, 3)
                for c in range(TILES - LEAST):
                    pool.dma_start(x_rows[SPARE + c * S:SPARE + (c + 1) * S, :].rearrange("(h p) w -> p h w", p=P),
                                   padrow[:, :, :]).then_inc(spare_st, 16)
                pool.dma_start(out[NP:NP + S, :].rearrange("(h p) d -> p h d", p=P),
                               padrow[:, :, 0:D]).then_inc(spare_st, 16)
                pool.wait_ge(even_lo, PAIRS)
                pool.sem_inc(w_lo, 2)

                def body(r, weights):
                    for s in range(2):
                        i = 2 * r + s
                        for u in ((2 * s, 2 * s + 1) if weights else ()):
                            e = r - 1
                            pool.wait_ge(w_hi, 4 * e + u + 1)
                            src = wst[:, u % 2, :] if u < KD else \
                                wst[:, u % 2, :].rearrange("p (c d) -> p c d", c=4)
                            if u < KD:
                                hi, lo = (w1s[:, bass.ds(e, 1), a, u, :].rearrange("p a h -> p (a h)")
                                          for a in range(2))
                            else:
                                c = (u - KD) * 4
                                hi, lo = (w2s[:, bass.ds(e, 1), c:c + 4, a, :].rearrange("p a c d -> p (a c) d")
                                          for a in range(2))
                            nc.gpsimd.tensor_tensor(lo, src, hi, ALU.subtract).then_inc(w_lo, 1)
                        if not (isinstance(i, int) and i < 2):
                            dispatch(i - 2, s)

                def dispatch(i, s):
                    pool.wait_ge(pos_rdy, i + 1)
                    for c in range(TOPK):
                        hold(pool)
                        nc.gpsimd.indirect_dma_start(
                            out=x_rows, out_offset=bass.IndirectOffsetOnAxis(ap=pos[:, s, c:c + 1].bitcast(u32), axis=0),
                            in_=row[:, s, :], in_offset=None).then_inc(sent[s], 16)

                pairs(pool, body)
                dispatch(NT - 2, 0)
                dispatch(NT - 1, 1)
                pool.wait_ge(spare_st, 16 * (TILES - LEAST + 1))
                for s in range(2):
                    pool.wait_ge(sent[s], 16 * NT)

            steps = [0]

            def slot_constants(dve):
                dve.wait_ge(w_lo, 2 + 4 * E)
                nc.vector.tensor_scalar(thr[:, :], iota_t[:, 0:KT], float(S), None, ALU.mult).then_inc(tstep, 1)
                nc.vector.memset(one_e[:, :], 1.0).then_inc(tstep, 1)
                nc.vector.memset(code[:, TILES:TILES + 1], 0).then_inc(tstep, 1)
                nc.vector.tensor_scalar(half_at, iota_t[:, :], float(S), float(P), ALU.mult, ALU.add) \
                    .then_inc(tstep, 1)
                steps[0] = 4

            def slot_tables(dve):
                def step(ins):
                    steps[0] += 1
                    ins.then_inc(tstep, 1)
                    dve.wait_ge(tstep, steps[0])

                def over(ap, n, pattern):
                    return ap.rearrange(pattern, **{"z": 1}).to_broadcast(n)

                dve.wait_ge(tstep, steps[0])
                counts = cmp_n[:, :, 0:KT]
                step(nc.vector.tensor_tensor(counts, over(total_ps, (P, E, KT), "p (e z) -> p e z"),
                                             over(thr[:, :], (P, E, KT), "p (z k) -> p z k"), ALU.is_gt))
                step(nc.vector.tensor_reduce(filled[:, :], counts, axis=AX.X, op=ALU.add))
                step(nc.vector.tensor_tensor_scan(cum[:, :], one_e[:, :], filled[:, :], 0.0, ALU.mult, ALU.add))
                step(nc.vector.tensor_tensor(cmp_t, over(iota_t[:, :], (P, TILES, E), "p (t z) -> p t z"),
                                             over(cum[:, :], (P, TILES, E), "p (z e) -> p z e"), ALU.is_ge))
                step(nc.vector.tensor_reduce(e_raw, cmp_t, axis=AX.X, op=ALU.add))
                step(nc.vector.tensor_tensor(cmp_w, cmp_t, over(filled[:, :], (P, TILES, E), "p (z e) -> p z e"),
                                             ALU.mult))
                step(nc.vector.tensor_reduce(start_t, cmp_w, axis=AX.X, op=ALU.add))
                step(nc.vector.tensor_tensor(start_t, iota_t[:, :], start_t, ALU.subtract))
                step(nc.vector.tensor_scalar(base_f, e_raw, float(CAP), None, ALU.mult))
                step(nc.vector.scalar_tensor_tensor(base_i[:, :], start_t, float(S), base_f, ALU.mult, ALU.add))
                step(nc.vector.tensor_scalar(e_f[:, :], e_raw, float(E - 1), None, ALU.min))
                step(nc.vector.tensor_copy(e_i[:, :], e_f[:, :]))
                step(nc.vector.tensor_copy(used_i, cum[:, E - 1:E]))
                step(nc.vector.tensor_tensor(start_e, cum[:, :], filled[:, :], ALU.subtract))
                step(nc.vector.scalar_tensor_tensor(end_e, start_e, float(S), total_ps, ALU.mult, ALU.add))
                step(nc.vector.tensor_tensor(cmp_w, over(half_at, (P, TILES, E), "p (t z) -> p t z"),
                                             over(end_e, (P, TILES, E), "p (z e) -> p z e"), ALU.is_lt))
                step(nc.vector.tensor_reduce(ends, cmp_w, axis=AX.X, op=ALU.add))
                step(nc.vector.tensor_scalar(base_f, e_raw, float(1 - E), float(E * E), ALU.mult, ALU.add))
                step(nc.vector.scalar_tensor_tensor(code[:, 0:TILES], ends, -float(E), base_f, ALU.mult, ALU.add))

            @block.vector
            def _(dve):
                begun = [0]

                def statistics_x(t1):
                    t0, begun[0] = begun[0], t1
                    for t in range(t0, t1 + 1):
                        if t < t1:
                            if t in XCUT:
                                dve.wait_ge(x_in[XCUT.index(t)], 16 if t < NT - 1 else 32)
                            nc.vector.bn_stats(stats_x[:, t, :], x_all[:, t, :]).then_inc(stats1, 1)
                        if t > t0:
                            dve.wait_ge(stats1, t)
                            nc.vector.bn_aggr(mv_x[:, t - 1, :], stats_x[:, t - 1, :]).then_inc(mv1, 1)

                def shifts(q):
                    t0, t1 = XPARTS[q]
                    dve.wait_ge(sd1, q + 1)
                    nc.vector.reciprocal(rstd_x[:, t0:t1], sd_x[:, t0:t1]).then_inc(rstd1, 1)
                    dve.wait_ge(rstd1, q + 1)
                    nc.vector.scalar_tensor_tensor(shift_x[:, t0:t1], mv_x[:, t0:t1, 0], -1.0, rstd_x[:, t0:t1],
                                                   ALU.mult, ALU.mult).then_inc(shift1, 1)

                def hidden_pair(j):
                    if j < PAIRS:
                        dve.wait_ge(wrow_ld, 16)
                        nc.vector.scalar_tensor_tensor(x_all[:, 2 * j, :], x_all[:, 2 * j, :],
                                                       mv_x[:, 2 * j, 0:1], wrow[:, :], ALU.subtract,
                                                       ALU.mult).then_inc(centred, 1)
                    if j:
                        t = 2 * j - 2
                        dve.wait_ge(even_hi, j)
                        nc.vector.scalar_tensor_tensor(hid[:, t, 1, :], x_all[:, t, :], rstd_x[:, t:t + 1],
                                                       hid[:, t, 0, :], ALU.mult, ALU.subtract).then_inc(even_lo, 1)

                def body(r, weights):
                    for s in range(2):
                        i = 2 * r + s
                        first = isinstance(i, int) and i == 0
                        second = isinstance(i, int) and i < 2
                        for g, (b0, nb) in enumerate(GROUPS):
                            n = NG * i + g
                            if first:
                                for what, n0 in HIDDEN_BY[g]:
                                    if what == "stats":
                                        statistics_x(n0)
                                    elif what == "root":
                                        shifts(n0)
                                    else:
                                        hidden_pair(n0)
                            dve.wait_ge(adj_hi, n + 1)
                            nc.vector.scalar_tensor_tensor(adjT[:, g % NBUF, 1, 0:nb * P], tp[g % 2][:, 0:nb * P],
                                                           S_ADJ, adjT[:, g % NBUF, 0, 0:nb * P], ALU.mult,
                                                           ALU.subtract).then_inc(adj_lo, 1)
                            if g == 0 and not second:
                                choose(i - 2, s)
                            if g == 1 and not first:
                                residual(i - 1, 1 - s, r if s else r - 1)
                            if g == 2 and not first:
                                statistics(i - 1, 1 - s)
                            if g == 0 and not second:
                                mark(i - 2, s)
                            if isinstance(i, int) and i == 1 and g == 3:
                                dve.wait_ge(const_set, 3)
                                dve.wait_ge(const_ld, 48)
                            if g == 3 and not first:
                                normalise(i - 1, 1 - s, r if s else r - 1)
                            if g == 4 and not second:
                                positions(i - 2, s)

                def residual(i, s, turn):
                    dve.wait_ge(mm_done, NG * (i + 1))
                    dve.wait_ge(xin_ld[s], 16 * turn + 16 * two(i))
                    scale = 1.0 / (S_ADJ * S_HID)
                    nc.vector.scalar_tensor_tensor(xin[:, s, :], acc[s][:, 0, :], scale, xin[:, s, :], ALU.mult,
                                                   ALU.add).then_inc(x1a, 1)
                    dve.wait_ge(x1a, i + 1)
                    nc.vector.scalar_tensor_tensor(xin[:, s, :], acc[s][:, 1, :], scale, xin[:, s, :], ALU.mult,
                                                   ALU.add).then_inc(x1b, 1)

                def statistics(i, s):
                    dve.wait_ge(x1b, i + 1)
                    hold(dve)
                    nc.vector.bn_stats(stats[:, :], xin[:, s, :]).then_inc(st2, 1)
                    dve.wait_ge(st2, i + 1)
                    hold(dve)
                    nc.vector.bn_aggr(mv[:, :], stats[:, :]).then_inc(mv2, 1)

                def normalise(i, s, turn):
                    dve.wait_ge(sd2, i + 1)
                    nc.vector.reciprocal(rstd[:, :], sd[:, :]).then_inc(rstd2, 1)
                    dve.wait_ge(rstd2, i + 1)
                    need(dve, sent[s], 32 * turn)
                    nc.vector.tensor_scalar(row[:, s, 0:D], xin[:, s, :], mv[:, 0:1], rstd[:, :], ALU.subtract,
                                            ALU.mult).then_inc(norm2, 1)
                    nc.vector.tensor_copy(row[:, s, C_TOK:XW], tok[:, bass.ds(i, 1)]).then_inc(tok_rdy, 1)

                def choose(i, s):
                    dve.wait_ge(gate_done, i + 1)
                    nc.vector.tensor_tensor(score[:, :], scores_ps, bgs[:, :], ALU.add).then_inc(sc_rdy, 1)
                    dve.wait_ge(sc_rdy, i + 1)
                    hold(dve)
                    nc.vector.max(top[:, :], score[:, :]).then_inc(top_rdy, 1)
                    dve.wait_ge(top_rdy, i + 1)
                    nc.vector.tensor_scalar(below[:, :], score[:, :], top[:, 0:1], None, ALU.subtract) \
                        .then_inc(below_rdy, 1)
                    nc.vector.max_index(topix[:, :], top[:, :], score[:, :]).then_inc(ix_rdy, 1)
                    dve.wait_ge(ix_rdy, i + 1)
                    nc.vector.tensor_copy(topf[:, :], topix[:, 0:TOPK]).then_inc(ixf_rdy, 1)
                    dve.wait_ge(ixf_rdy, i + 1)
                    nc.vector.tensor_tensor(row[:, s, C_ELO:C_ELO + 1], topf[:, 0:1], topf[:, 1:2], ALU.min) \
                        .then_inc(e_rdy, 1)
                    nc.vector.tensor_tensor(ehi[:, :], topf[:, 0:1], topf[:, 1:2], ALU.max).then_inc(e_rdy, 1)

                def mark(i, s):
                    dve.wait_ge(e_rdy, 2 * i + 2)
                    for c, which in enumerate((row[:, s, C_ELO:C_ELO + 1], ehi[:, :])):
                        nc.vector.tensor_scalar(hot[:, c, :], iota_e[:, :], which, live[:, bass.ds(i, 1)],
                                                ALU.is_equal, ALU.mult).then_inc(hot_rdy, 1)
                    dve.wait_ge(hot_rdy, 2 * i + 2)
                    nc.vector.tensor_tensor(both[:, :], hot[:, 0, :], hot[:, 1, :], ALU.add).then_inc(both_rdy, 1)
                    dve.wait_ge(below_rdy, i + 1)
                    for c in range(TOPK):
                        nc.vector.scalar_tensor_tensor(junk[:, c, :], hot[:, c, :], 1.0, below[:, :], ALU.mult,
                                                       ALU.mult, accum_out=row[:, s, C_SLO + c:C_SLO + c + 1]) \
                            .then_inc(slo_rdy, 1)
                    dve.wait_ge(both_rdy, i + 1)
                    nc.vector.tensor_tensor(count[:, 1 - s, :], count[:, s, :], both[:, :], ALU.add) \
                        .then_inc(count_rdy, 1)

                def positions(i, s):
                    dve.wait_ge(rank_done, i + 1)
                    nc.vector.tensor_tensor(place[:, :], rank_ps, region[:, :], ALU.add).then_inc(place_rdy, 1)
                    dve.wait_ge(place_rdy, i + 1)
                    for c in range(TOPK):
                        nc.vector.scalar_tensor_tensor(junk[:, c, :], hot[:, c, :], 1.0, place[:, :], ALU.mult,
                                                       ALU.mult, accum_out=posf[:, c:c + 1]).then_inc(posf_rdy, 1)
                    dve.wait_ge(posf_rdy, 2 * i + 2)
                    dve.wait_ge(slo_rdy, 2 * i + 2)
                    dve.wait_ge(tok_rdy, i + 1)
                    nc.vector.tensor_tensor(pos[:, s, :], posf[:, :],
                                            dump[:, bass.ds(i, 1), :].rearrange("p a c -> p (a c)"),
                                            ALU.add).then_inc(pos_rdy, 1)

                pairs(dve, body)
                choose(NT - 2, 0)
                mark(NT - 2, 0)
                residual(NT - 1, 1, PAIRS - 1)
                statistics(NT - 1, 1)
                normalise(NT - 1, 1, PAIRS - 1)
                positions(NT - 2, 0)
                slot_constants(dve)
                choose(NT - 1, 1)
                mark(NT - 1, 1)
                dve.wait_ge(total_done, 1)
                nc.vector.tensor_tensor(padat[:, :], total_ps, region[:, :], ALU.add).then_inc(pads_known, 1)
                positions(NT - 1, 1)
                slot_tables(dve)

            @block.tensor
            def _(pe):
                def turn_adj(i, s, g, r):
                    b0, nb = GROUPS[g]
                    n = NG * i + g
                    if isinstance(i, int) and i == 0:
                        pe.wait_ge(adj_first if g < AHEAD else adj_ld[0], 16)
                    elif g == 0:
                        pe.wait_ge(adj_ld[s], 16 * r + 16 * two(i))
                    need(pe, adj_lo, n - 1)
                    for b in range(nb):
                        last = nc.tensor.transpose(tp[g % 2][:, b * P:(b + 1) * P],
                                                   adj_in[:, s, (b0 + b) * P:(b0 + b + 1) * P], ident[:, :])
                    last.then_inc(tposed, 1)

                def product(i, s, g):
                    b0, nb = GROUPS[g]
                    pe.wait_ge(adj_lo, NG * i + g + 1)
                    if isinstance(i, int) and i == 0:
                        pe.wait_ge(even_lo, (b0 + nb + 1) // 2)
                        pe.wait_ge(odd_lo, (b0 + nb) // 2)
                    if g == 0:
                        need(pe, x1b, i - 1)
                    for b in range(nb):
                        blk = b0 + b
                        nc.tensor.matmul(acc[s][:, :, :], adjT[:, g % NBUF, 0, b * P:(b + 1) * P],
                                         hid[:, blk, :, :], start=(blk == 0), stop=False, skip_group_check=True)
                        last = nc.tensor.matmul(acc[s][:, 1, :], adjT[:, g % NBUF, 1, b * P:(b + 1) * P],
                                                hid[:, blk, 0, :], start=False, stop=(blk == NT - 1),
                                                skip_group_check=True)
                    last.then_inc(mm_done, 1)

                def turn_norm(i, s):
                    pe.wait_ge(norm2, i + 1)
                    need(pe, nT_rdy, i)
                    for k in range(KD):
                        last = nc.tensor.transpose(small[:, k * P:(k + 1) * P], row[:, s, k * P:(k + 1) * P],
                                                   ident[:, :])
                    last.then_inc(nT_done, 1)

                def gate(i):
                    pe.wait_ge(nT_rdy, i + 1)
                    need(pe, sc_rdy, i)
                    need(pe, place_rdy, i)
                    for k in range(KD):
                        last = nc.tensor.matmul(scores_ps, x1T[:, k, :], wgs[:, k, :], start=(k == 0),
                                                stop=(k == KD - 1))
                    last.then_inc(gate_done, 1)

                def rank(i, s):
                    pe.wait_ge(both_rdy, i + 1)
                    need(pe, count_rdy, i)
                    need(pe, place_rdy, i)
                    nc.tensor.matmul(rank_ps, before[:, :], both[:, :], start=True, stop=False)
                    nc.tensor.matmul(rank_ps, ones[:, :], count[:, s, :], start=False, stop=True) \
                        .then_inc(rank_done, 1)

                def body(r, weights):
                    for s in range(2):
                        i = 2 * r + s
                        first = isinstance(i, int) and i == 0
                        final = isinstance(i, int) and i == NT - 1
                        for g in range(NG):
                            if g + AHEAD < NG:
                                turn_adj(i, s, g + AHEAD, r)
                            elif not final:
                                turn_adj(i + 1, 1 - s, g + AHEAD - NG, r + s)
                            if not first:
                                if g == 4:
                                    turn_norm(i - 1, 1 - s)
                                if g == 5:
                                    gate(i - 1)
                            if g == 3 and not (isinstance(i, int) and i < 2):
                                rank(i - 2, s)
                            product(i, s, g)

                pe.wait_ge(ident_rdy, 2)
                for g in range(AHEAD):
                    turn_adj(0, 0, g, 0)
                body(0, False)
                with pe.Fori(1, PAIRS - 1) as r:
                    body(r, False)
                body(PAIRS - 1, False)
                rank(NT - 2, 0)
                turn_norm(NT - 1, 1)
                gate(NT - 1)
                pe.wait_ge(count_rdy, NT)
                nc.tensor.matmul(total_ps, ones[:, :], count[:, NT % 2, :], start=True, stop=True) \
                    .then_inc(total_done, 1)
                rank(NT - 1, 1)

        with nc.Block() as block:

            @block.sync
            def _(sp):
                def load_b2(t, s):
                    need(sp, yb_rdy, NH * (t - 1))
                    hold(sp)
                    e = sp.value_load(e_i[0:1, bass.ds(t, 1)], min_val=0, max_val=E - 1)
                    sp.dma_start(b2t[:, s, :], b2[bass.ds(e, 1), :].to_broadcast((P, D))).then_inc(b2_ld[s], 16)

                def load_rows_of(t, s):
                    need(sp, xT_done, t - 1)
                    need(sp, meta_rdy, t - 1)
                    r0 = sp.value_load(base_i[0:1, bass.ds(t, 1)], min_val=0, max_val=XROWS - TOPK - S)
                    if isinstance(t, int) and t == 0:
                        sp.wait_ge(pad_st, 16 * E)
                    sp.dma_start(xr[:, s, :, :], x_rows[bass.ds(r0, S), :].rearrange("(h p) w -> p h w", p=P)) \
                        .then_inc(xr_ld[s], 16)

                def body(t, s, q, have):
                    with have(t) as u:
                        load_rows_of(u, s)
                    if there(t - 1):
                        with have(t - 1) as u:
                            load_b2(u, 1 - s)

                tiles(sp, body)
                used = sp.value_load(used_i[0:1, 0:1], min_val=LEAST, max_val=TILES)
                sp.wait_ge(z_st, used * (16 * NH))
                hold(sp)

            @block.scalar
            def _(act):
                nc.scalar.activation(sd[:, :], sd[:, :], ACT.Exp)
                act.wait_ge(b1_done, 1)
                nc.scalar.activation(b1t[:, :], b1_ps, ACT.Copy, scale=S_H).then_inc(b1_rdy, 1)

                def x_hi(t, s):
                    act.wait_ge(xT_done, t + 1)
                    need(act, h_done, KB * (t - 1))
                    nc.scalar.activation(xT[:, s, 0, :, :], xT_ps, ACT.Copy, scale=S_X).then_inc(xT_hi, 1)

                def hidden_hi(t, s):
                    for a in range(KB):
                        act.wait_ge(h32_rdy, KB * t + a + 1)
                        need(act, y_done, NH * (t - 1))
                        nc.scalar.activation(hsp[:, s, 0, 2 * a:2 * a + 2, :], h32[:, a, :, :], ACT.Relu) \
                            .then_inc(h_hi, 1)

                def copy_meta(t, s):
                    need(act, zi_rdy, t - 1)
                    need(act, high_rdy, t - 1)
                    nc.scalar.activation(meta[:, s, :, :], xr[:, s, :, D:XW], ACT.Copy).then_inc(meta_rdy, 1)

                def exps(t, s):
                    need(act, ssum_rdy, t - 1)
                    need(act, wn_rdy, t - 1)
                    act.wait_ge(meta_rdy, t + 1)
                    nc.scalar.activation(sexp[:, s, :, :], meta[:, s, :, 0:TOPK], ACT.Exp).then_inc(sexp_rdy, 1)

                def weigh(t, s):
                    for h in range(NH):
                        act.wait_ge(yb_rdy, NH * t + h + 1)
                        act.wait_ge(wt_rdy, t + 1)
                        need(act, z_st, 16 * NH * (t - 1))
                        nc.scalar.activation(yrow[:, s, h, :], ysum[:, h, :], ACT.Copy, scale=wt[:, s, h:h + 1]) \
                            .then_inc(y_rdy, 1)

                def body(t, s, q, have):
                    if there(t - 1):
                        with have(t - 1) as u:
                            weigh(u, 1 - s)
                    with have(t + 2) as u:
                        x_hi(u, s)
                        copy_meta(u, s)
                    with have(t + 1) as u:
                        exps(u, 1 - s)
                        hidden_hi(u, 1 - s)

                for t in range(2):
                    x_hi(t, t)
                    copy_meta(t, t)
                exps(0, 0)
                hidden_hi(0, 0)
                tiles(act, body)

            @block.gpsimd
            def _(pool):
                def gate_weights(t, s):
                    pool.wait_ge(meta_rdy, t + 1)
                    need(pool, z_st, 16 * NH * (t - 1))
                    hold(pool)
                    nc.gpsimd.tensor_copy(zi[:, s, :], meta[:, s, :, C_TOK - D]).then_inc(zi_rdy, 1)
                    pool.wait_ge(sexp_rdy, t + 1)
                    nc.gpsimd.tensor_tensor(wd[:, s, :], sexp[:, s, :, 1], sexp[:, s, :, 0], ALU.subtract) \
                        .then_inc(wd_rdy, 1)
                    nc.gpsimd.tensor_tensor(ssum[:, s, :], sexp[:, s, :, 1], sexp[:, s, :, 0], ALU.add) \
                        .then_inc(ssum_rdy, 1)
                    pool.wait_ge(wd_rdy, t + 1)
                    pool.wait_ge(high_rdy, t + 1)
                    nc.gpsimd.tensor_tensor(wf[:, s, :], wd[:, s, :], high[:, s, :], ALU.mult).then_inc(wf_rdy, 1)
                    pool.wait_ge(wf_rdy, t + 1)
                    need(pool, wt_rdy, t - 1)
                    nc.gpsimd.tensor_tensor(wn[:, s, :], wf[:, s, :], sexp[:, s, :, 0], ALU.add).then_inc(wn_rdy, 1)

                def scatter(t, s):
                    for h in range(NH):
                        pool.wait_ge(y_rdy, NH * t + h + 1)
                        if h == 0:
                            need(pool, z_st, 16 * NH * t)
                        hold(pool)
                        nc.gpsimd.indirect_dma_start(
                            out=out, out_offset=bass.IndirectOffsetOnAxis(ap=zi[:, s, h:h + 1].bitcast(u32), axis=0),
                            in_=yrow[:, s, h, :], in_offset=None, compute_op=ALU.add).then_inc(z_st, 16)

                def body(t, s, q, have):
                    if there(t - 1):
                        with have(t - 1) as u:
                            scatter(u, 1 - s)
                    with have(t + 1) as u:
                        gate_weights(u, 1 - s)

                gate_weights(0, 0)
                tiles(pool, body)

            @block.vector
            def _(dve):
                def x_lo(t, s):
                    dve.wait_ge(xT_hi, t + 1)
                    nc.vector.scalar_tensor_tensor(xT[:, s, 1, :, :], xT_ps, S_X, xT[:, s, 0, :, :], ALU.mult,
                                                   ALU.subtract).then_inc(xT_lo, 1)

                def which(t, s):
                    dve.wait_ge(meta_rdy, t + 1)
                    need(dve, wf_rdy, t - 1)
                    nc.vector.tensor_scalar(high[:, s, :], meta[:, s, :, C_ELO - D], e_f[:, bass.ds(t, 1)], None,
                                            ALU.is_lt).then_inc(high_rdy, 1)

                def hidden(t, s):
                    e = dve.value_load(e_i[0:1, bass.ds(t, 1)], min_val=0, max_val=E - 1)

                    def bias(a):
                        dve.wait_ge(h_done, KB * t + a + 1)
                        need(dve, h_lo, KB * (t - 1) + a + 1)
                        nc.vector.scalar_tensor_tensor(
                            h32[:, a, :, :], h_ps[a], S_H / (S_X * S_W),
                            b1t[:, bass.ds(e * KH + 2 * a, 2)].rearrange("p (c z) -> p c z", z=1)
                            .to_broadcast((P, 2, S)), ALU.mult, ALU.add).then_inc(h32_rdy, 1)

                    def low(a):
                        dve.wait_ge(h_hi, KB * t + a + 1)
                        nc.vector.scalar_tensor_tensor(
                            hsp[:, s, 1, 2 * a:2 * a + 2, :], h32[:, a, :, :], 0.0,
                            hsp[:, s, 0, 2 * a:2 * a + 2, :], ALU.max, ALU.subtract).then_inc(h_lo, 1)

                    for a in range(KB):
                        bias(a)
                        if a >= 2:
                            low(a - 2)
                    for a in range(KB - 2, KB):
                        low(a)

                def weights(t, s):
                    dve.wait_ge(ssum_rdy, t + 1)
                    nc.vector.reciprocal(srec[:, s, :], ssum[:, s, :]).then_inc(srec_rdy, 1)
                    dve.wait_ge(srec_rdy, t + 1)
                    dve.wait_ge(wn_rdy, t + 1)
                    need(dve, y_rdy, NH * (t - 1))
                    nc.vector.tensor_tensor(wt[:, s, :], wn[:, s, :], srec[:, s, :], ALU.mult).then_inc(wt_rdy, 1)

                def result(t, s, q):
                    dve.wait_ge(b2_ld[s], 16 * (q + 1))
                    for h in range(NH):
                        dve.wait_ge(y_done, NH * t + h + 1)
                        need(dve, y_rdy, NH * (t - 1) + h + 1)
                        nc.vector.scalar_tensor_tensor(ysum[:, h, :], acc[h][:, 0, :], 1.0 / (S_H * S_W),
                                                       b2t[:, s, :], ALU.mult, ALU.add).then_inc(ya_rdy, 1)
                        dve.wait_ge(ya_rdy, NH * t + h + 1)
                        nc.vector.scalar_tensor_tensor(ysum[:, h, :], acc[h][:, 1, :], 1.0 / (S_H * S_W),
                                                       ysum[:, h, :], ALU.mult, ALU.add).then_inc(yb_rdy, 1)

                def body(t, s, q, have):
                    if there(t - 1):
                        with have(t - 1) as u:
                            result(u, 1 - s, q + s - 1)
                    with have(t + 2) as u:
                        x_lo(u, s)
                    with have(t) as u:
                        weights(u, s)
                    with have(t + 1) as u:
                        hidden(u, 1 - s)
                        which(u, 1 - s)

                x_lo(0, 0)
                x_lo(1, 1)
                dve.wait_ge(b1_rdy, 1)
                hidden(0, 0)
                which(0, 0)
                tiles(dve, body)

            @block.tensor
            def _(pe):
                nc.tensor.transpose(b1_ps, b1r[:, :], ident[0:E * KH, 0:E * KH]).then_inc(b1_done, 1)

                def turn(t, s, q):
                    pe.wait_ge(xr_ld[s], 16 * (q + 1))
                    need(pe, xT_lo, t)
                    for k in range(KD):
                        for h in range(NH):
                            last = nc.tensor.transpose(xT_ps[:, k, h * P:(h + 1) * P],
                                                       xr[:, s, h, k * P:(k + 1) * P], ident[:, :])
                    last.then_inc(xT_done, 1)

                def load_code(t):
                    if isinstance(t, int) and t == 0:
                        return pe.value_load(e_i[0:1, 0:1], min_val=0, max_val=E - 1)
                    return pe.value_load(code[0:1, bass.ds(t, 1)], min_val=0, max_val=2 * E - 1)

                def in_halves(t, v, product):
                    if isinstance(t, int) and t == 0:
                        product(v, NH)
                        return
                    with pe.If(v < E):
                        product(v.with_bounds(min_val=0, max_val=E - 1), NH)
                    with pe.Else():
                        product((v - E).with_bounds(min_val=0, max_val=E - 1), 1)

                def up(t, s, v):
                    in_halves(t, v, lambda e, halves: up_halves(t, s, e, halves))

                def down(t, s, v):
                    in_halves(t, v, lambda e, halves: down_halves(t, s, e, halves))

                def up_halves(t, s, e, halves):
                    slots = slice(0, halves * P)
                    pe.wait_ge(xT_lo, t + 1)
                    for c in range(KH):
                        if c % 2 == 0:
                            need(pe, h32_rdy, KB * (t - 1) + c // 2 + 1)
                        for k in range(KD):
                            for n, (wv, xv) in enumerate(((0, 0), (0, 1), (1, 0))):
                                w = w1s[:, bass.ds(e, 1), wv, k, c * P:(c + 1) * P].rearrange("p a n -> p (a n)")
                                last = nc.tensor.matmul(h_ps[c // 2][:, c % 2, slots], w, xT[:, s, xv, k, slots],
                                                        start=(k == 0 and n == 0), stop=(k == KD - 1 and n == 2))
                        if c % 2:
                            last.then_inc(h_done, 1)

                def down_halves(t, s, e, halves):
                    for c in range(KH):
                        if c % 2 == 0:
                            pe.wait_ge(h_lo, KB * t + c // 2 + 1)
                        w = w2s[:, bass.ds(e, 1), c, :, :].rearrange("p a v d -> p (a v) d")
                        for h in range(halves):
                            if c == 0:
                                need(pe, yb_rdy, NH * (t - 1) + h + 1)
                            at = slice(h * P, (h + 1) * P)
                            nc.tensor.matmul(acc[h][:, :, :], hsp[:, s, 0, c, at], w, start=(c == 0), stop=False,
                                             skip_group_check=True)
                            last = nc.tensor.matmul(acc[h][:, 1, :], hsp[:, s, 1, c, at], w[:, 0, :], start=False,
                                                    stop=(c == KH - 1), skip_group_check=True)
                            if c == KH - 1:
                                last.then_inc(y_done, NH // halves)

                def body(t, s, q, have):
                    with have(t + 2) as u:
                        turn(u, s, q + 1)
                    v = load_code(t)
                    with have(t + 1) as u:
                        up(u, 1 - s, load_code(u))
                    with have(t) as u:
                        down(u, s, v)

                for _ in range(BUSY):
                    nc.tensor.transpose(xT_ps[:, 0, 0:P], ident[:, :], ident[:, :])
                turn(0, 0, 0)
                turn(1, 1, 0)
                pe.wait_ge(b1_rdy, 1)
                up(0, 0, load_code(0))
                tiles(pe, body)


_INS = ["x", "adj", "L0_gnn_W", "L0_ffn_W1", "L0_ffn_b1", "L0_ffn_W2", "L0_ffn_b2", "L0_ffn_Wg", "L0_ffn_bg"]
_OUTS = [((OROWS, D), "float32")]


def kernel(**inputs):
    import numpy as _np
    import concourse.bacc as _bacc
    from concourse import mybir as _mybir
    from concourse.bass_utils import run_bass_kernel_spmd as _run

    nc = _bacc.Bacc("TRN2", target_bir_lowering=False, num_devices=1)
    arrays, args = {}, []
    for name in _INS:
        a = _np.ascontiguousarray(inputs[name])
        arrays[f"in_{name}_dram"] = a
        args.append(nc.dram_tensor(f"in_{name}_dram", a.shape, _mybir.dt.from_np(a.dtype), kind="ExternalInput").ap())
    for i, (shape, dtype) in enumerate(_OUTS):
        dt = _mybir.dt.from_np(_np.dtype(dtype))
        args.append(nc.dram_tensor(f"out_{i}_dram", shape, dt, kind="ExternalOutput").ap())
    gnn_moe(nc, *args)
    r = _run(nc, [arrays], core_ids=[0])
    return r.results[0]["out_0_dram"][0:N]
```
